# Optimizing a Trainium2 kernel written in Bass

```python
import numpy as np
import jax
import jax.numpy as jnp

def _softmax(x, axis=-1):
    return jax.nn.softmax(x, axis=axis)

def _gelu(x):
    return jax.nn.gelu(x, approximate=True)

def _silu(x):
    return jax.nn.silu(x)

def _sigmoid(x):
    return jax.nn.sigmoid(x)

def _layernorm(x, axis=-1, eps=1e-05):
    m = jnp.mean(x, axis=axis, keepdims=True)
    v = jnp.var(x, axis=axis, keepdims=True)
    return (x - m) / jnp.sqrt(v + eps)

def _scatter_add(tgt, idx, src, axis=0):
    return tgt.at[idx].add(src)

def _segment_sum(src, seg, n):
    return jax.ops.segment_sum(src, seg, n)
kernel_name = 'mk_recurrent_d1_jaxref_r8_8e566e'

def setup_inputs(seed: int=0):
    np.random.seed(seed)
    _w = jnp.asarray

    def _L0_attn_setup():
        import math
        import jax, jax.numpy as jnp
        import numpy as np
        HIDDEN = 128
        NUM_HEADS = 16
        NUM_QUERIES = 2
        NUM_Q_HEADS = NUM_HEADS * NUM_QUERIES
        HEAD_DIM = 64
        Q_DIM = NUM_Q_HEADS * HEAD_DIM
        KV_DIM = NUM_HEADS * HEAD_DIM
        BATCH, SEQ = (4, 128)

        def _alibi_slopes(num_heads: int) -> np.ndarray:
            closest_pow2 = 2 ** int(math.floor(math.log2(num_heads)))
            base = 2.0 ** (-2.0 ** (-(math.log2(closest_pow2) - 3)))
            powers = np.arange(1, closest_pow2 + 1, dtype=np.float32)
            slopes = base ** powers
            if closest_pow2 != num_heads:
                extra_base = 2.0 ** (-2.0 ** (-(math.log2(2 * closest_pow2) - 3)))
                extra_powers = np.arange(1, 2 * (num_heads - closest_pow2) + 1, 2, dtype=np.float32)
                slopes = np.concatenate([slopes, extra_base ** extra_powers])
            return slopes[:num_heads].astype(np.float32)
        ALIBI_SLOPES = jnp.asarray(_alibi_slopes(NUM_Q_HEADS))
        key = jax.random.key(seed)
        k1, k2, k3 = jax.random.split(key, 3)
        inputs = jax.random.normal(k1, (BATCH, SEQ, HIDDEN), dtype=jnp.float32)
        W_qkv = jax.random.normal(k2, (HIDDEN, Q_DIM + 2 * KV_DIM), dtype=jnp.float32) * (1.0 / math.sqrt(HIDDEN))
        W_out = jax.random.normal(k3, (Q_DIM, HIDDEN), dtype=jnp.float32) * (1.0 / math.sqrt(Q_DIM))
        return {'inputs': inputs, 'W_qkv': W_qkv, 'W_out': W_out}
    _L0_attn_in = _L0_attn_setup()

    def _L0_ffn_setup():
        import jax, jax.numpy as jnp
        import numpy as np
        B, T, D = (2, 256, 128)
        E, K, FF = (8, 2, 512)

        def _reference_tuple_inner(x, gate_w, gate_b, w1, b1, w2, b2):
            n_experts = w1.shape[0]
            gate_logits = x @ gate_w + gate_b
            topk_vals, topk_idx = jax.lax.top_k(gate_logits, K)
            topk_w = jax.nn.softmax(topk_vals, axis=-1)
            onehot = jax.nn.one_hot(topk_idx, n_experts, dtype=x.dtype)
            comb = jnp.sum(onehot * topk_w[..., None], axis=2)
            h = jax.nn.gelu(jnp.einsum('btd,edf->ebtf', x, w1) + b1[:, None, None, :], approximate=False)
            y = jnp.einsum('ebtf,efd->ebtd', h, w2) + b2[:, None, None, :]
            output = jnp.einsum('ebtd,bte->btd', y, comb)
            expert_counts = jnp.sum(onehot, axis=(0, 1, 2)).astype(jnp.float32)
            return (output, gate_logits, topk_idx, expert_counts)
        key = jax.random.key(seed)
        ks = jax.random.split(key, 4)
        scale = 0.02
        return {'x': jax.random.normal(ks[0], (B, T, D), jnp.float32), 'gate_w': jax.random.normal(ks[1], (D, E), jnp.float32) * scale, 'gate_b': jnp.zeros((E,), jnp.float32), 'w1': jax.random.normal(ks[2], (E, D, FF), jnp.float32) * scale, 'b1': jnp.zeros((E, FF), jnp.float32), 'w2': jax.random.normal(ks[3], (E, FF, D), jnp.float32) * scale, 'b2': jnp.zeros((E, D), jnp.float32)}
    _L0_ffn_in = _L0_ffn_setup()
    _d = {'L0_attn_inputs': _L0_attn_in['inputs'], 'L0_attn_W_qkv': _L0_attn_in['W_qkv'], 'L0_attn_W_out': _L0_attn_in['W_out'], 'L0_ffn_gate_w': _L0_ffn_in['gate_w'], 'L0_ffn_gate_b': _L0_ffn_in['gate_b'], 'L0_ffn_w1': _L0_ffn_in['w1'], 'L0_ffn_b1': _L0_ffn_in['b1'], 'L0_ffn_w2': _L0_ffn_in['w2'], 'L0_ffn_b2': _L0_ffn_in['b2']}
    _x0 = _d['L0_attn_inputs']
    _d['L0_attn_inputs'] = jax.random.normal(jax.random.fold_in(jax.random.key(seed), 1), (8, 512, 128), dtype=_x0.dtype)
    del _x0
    return _d

def reference(L0_attn_inputs, L0_attn_W_qkv, L0_attn_W_out, L0_ffn_gate_w, L0_ffn_gate_b, L0_ffn_w1, L0_ffn_b1, L0_ffn_w2, L0_ffn_b2):

    def _L0_attn_ref(inputs, W_qkv, W_out):
        import math
        import jax, jax.numpy as jnp
        import numpy as np
        HIDDEN = 128
        NUM_HEADS = 16
        NUM_QUERIES = 2
        NUM_Q_HEADS = NUM_HEADS * NUM_QUERIES
        HEAD_DIM = 64
        Q_DIM = NUM_Q_HEADS * HEAD_DIM
        KV_DIM = NUM_HEADS * HEAD_DIM
        BATCH, SEQ = (4, 128)

        def _alibi_slopes(num_heads: int) -> np.ndarray:
            closest_pow2 = 2 ** int(math.floor(math.log2(num_heads)))
            base = 2.0 ** (-2.0 ** (-(math.log2(closest_pow2) - 3)))
            powers = np.arange(1, closest_pow2 + 1, dtype=np.float32)
            slopes = base ** powers
            if closest_pow2 != num_heads:
                extra_base = 2.0 ** (-2.0 ** (-(math.log2(2 * closest_pow2) - 3)))
                extra_powers = np.arange(1, 2 * (num_heads - closest_pow2) + 1, 2, dtype=np.float32)
                slopes = np.concatenate([slopes, extra_base ** extra_powers])
            return slopes[:num_heads].astype(np.float32)
        ALIBI_SLOPES = jnp.asarray(_alibi_slopes(NUM_Q_HEADS))
        B, S, _ = inputs.shape
        qkv = inputs @ W_qkv
        q = qkv[..., :Q_DIM].reshape(B, S, NUM_Q_HEADS, HEAD_DIM).transpose(0, 2, 1, 3)
        k = qkv[..., Q_DIM:Q_DIM + KV_DIM].reshape(B, S, NUM_HEADS, HEAD_DIM).transpose(0, 2, 1, 3)
        v = qkv[..., Q_DIM + KV_DIM:].reshape(B, S, NUM_HEADS, HEAD_DIM).transpose(0, 2, 1, 3)
        k = jnp.repeat(k, NUM_QUERIES, axis=1)
        v = jnp.repeat(v, NUM_QUERIES, axis=1)
        pos = jnp.arange(S)
        rel = (pos[None, :] - pos[:, None]).astype(jnp.float32)
        bias = ALIBI_SLOPES[:, None, None] * rel[None, :, :]
        scores = jnp.einsum('bhqd,bhkd->bhqk', q, k) / math.sqrt(HEAD_DIM)
        scores = scores + bias[None]
        causal = pos[:, None] >= pos[None, :]
        scores = jnp.where(causal[None, None], scores, -jnp.inf)
        attn = jax.nn.softmax(scores, axis=-1)
        out = jnp.einsum('bhqk,bhkd->bhqd', attn, v)
        out = out.transpose(0, 2, 1, 3).reshape(B, S, Q_DIM)
        return out @ W_out

    def _L0_ffn_ref(x, gate_w, gate_b, w1, b1, w2, b2):
        import jax, jax.numpy as jnp
        import numpy as np
        B, T, D = (2, 256, 128)
        E, K, FF = (8, 2, 512)

        def _reference_tuple_inner(x, gate_w, gate_b, w1, b1, w2, b2):
            n_experts = w1.shape[0]
            gate_logits = x @ gate_w + gate_b
            topk_vals, topk_idx = jax.lax.top_k(gate_logits, K)
            topk_w = jax.nn.softmax(topk_vals, axis=-1)
            onehot = jax.nn.one_hot(topk_idx, n_experts, dtype=x.dtype)
            comb = jnp.sum(onehot * topk_w[..., None], axis=2)
            h = jax.nn.gelu(jnp.einsum('btd,edf->ebtf', x, w1) + b1[:, None, None, :], approximate=False)
            y = jnp.einsum('ebtf,efd->ebtd', h, w2) + b2[:, None, None, :]
            output = jnp.einsum('ebtd,bte->btd', y, comb)
            expert_counts = jnp.sum(onehot, axis=(0, 1, 2)).astype(jnp.float32)
            return (output, gate_logits, topk_idx, expert_counts)
        return _reference_tuple_inner(x, gate_w, gate_b, w1, b1, w2, b2)[0]
    x = L0_attn_inputs
    xn = _layernorm(x, axis=-1)
    s = _L0_attn_ref(xn, L0_attn_W_qkv, L0_attn_W_out)
    g = _silu(_L0_ffn_ref(xn, L0_ffn_gate_w, L0_ffn_gate_b, L0_ffn_w1, L0_ffn_b1, L0_ffn_w2, L0_ffn_b2))
    x = x + s * g
    return x

_drawn_inputs = setup_inputs


def setup_inputs(seed=0):
    import zlib

    import numpy as np

    out = dict(_drawn_inputs(seed))
    spreads = {'L0_ffn_gate_b': (0.0, 0.761), 'L0_ffn_b1': (0.0, 0.8), 'L0_ffn_b2': (0.0, 0.641)}
    factors = {'L0_attn_W_qkv': 3.851,
     'L0_attn_W_out': 3.828,
     'L0_ffn_gate_w': 4.549,
     'L0_ffn_w1': 8.0,
     'L0_ffn_w2': 7.417}
    for name, (base, spread) in spreads.items():
        noise = np.random.default_rng([zlib.crc32(name.encode()), seed]).standard_normal(out[name].shape)
        drawn = base * np.exp(spread * noise) if base else spread * noise
        out[name] = jnp.asarray(drawn.astype(out[name].dtype))
    for name, factor in factors.items():
        out[name] = (out[name] * factor).astype(out[name].dtype)
    return out
```

```python
from contextlib import ExitStack

import numpy as np

import concourse.bass as bass
from concourse import mybir

F32 = mybir.dt.float32
F16 = mybir.dt.float16
BF16 = mybir.dt.bfloat16
ALU = mybir.AluOpType
ACT = mybir.ActivationFunctionType
AX_X = mybir.AxisListType.X

P = 128
NB, SEQ, D = 8, 512, 128
TOK = NB * SEQ
NT = TOK // P
QT = SEQ // P
E, FF = 8, 512
FC = FF // P
HQ, HKV, DH = 32, 16, 64
WS = 64.0
EPS = 1e-5
BIG = 1e30

GROUPS = [[(0, 3, 0)], [(0, 0, 0), (0, 2, 128)], [(0, 1, 0), (1, 1, 256)], [(1, 3, 0)],
          [(1, 0, 0), (1, 2, 128)]]
NG = len(GROUPS)
SLOTS = 2
GB = SLOTS * NG
BODIES = NB * HKV // SLOTS
PAIRS = HKV // SLOTS
LAG_T, LAG_PV = 2, 4
ON_ACT = (0, 2, 3)


def alibi_slopes():
    base = 2.0 ** (-2.0 ** (-(np.log2(HQ) - 3)))
    return (base ** np.arange(1, HQ + 1, dtype=np.float32)).astype(np.float32)


def build(nc, x, w_qkv, w_out, gate_w, gate_b, w1, b1, w2, b2, out):
    slopes = [float(s) for s in alibi_slopes()]
    ctx = ExitStack()
    with ctx:
        def sb(name, shape, dt):
            return ctx.enter_context(nc.sbuf_tensor(name, shape, dt))

        def sem(name):
            return ctx.enter_context(nc.semaphore(name))

        X = sb("X", [P, NT, D], F32)
        ident = sb("ident", [P, P], F32)
        relpos = sb("relpos", [P, SEQ], F32)
        nslope = sb("nslope", [P, HQ], F32)
        qscale = sb("qscale", [P, HQ], F32)
        xT_hi = sb("xT_hi", [P, TOK], F16)
        xT_lo = sb("xT_lo", [P, TOK], F16)
        w1_hi = sb("w1_hi", [P, E * FF], F16)
        w1_lo = sb("w1_lo", [P, E * FF], F16)
        w2_hi = sb("w2_hi", [P, E * FC, D], F16)
        w2_lo = sb("w2_lo", [P, E * FC, D], F16)
        wq_hi = sb("wq_hi", [P, HQ * DH], F16)
        wq_lo = sb("wq_lo", [P, HQ * DH], F16)
        wk_hi = sb("wk_hi", [P, HKV, 2, DH], F16)
        wk_lo = sb("wk_lo", [P, HKV, 2, DH], F16)
        wv_hi = sb("wv_hi", [P, HKV * DH], F16)
        wv_lo = sb("wv_lo", [P, HKV * DH], F16)
        wo_hi = sb("wo_hi", [P, HKV, D], F16)
        wo_lo = sb("wo_lo", [P, HKV, D], F16)
        mix = sb("mix", [P, NT, D], F32)
        att = sb("att", [P, NT, D], F32)
        b2_row = sb("b2_row", [P, E, QT, D], F16)
        ones = sb("ones", [P, P], F16)
        NSTG, CH = 4, 2048
        stage = sb("stage", [P, NSTG, CH], F32)
        gw = sb("gw", [P, 2 * E], F32)
        gw16 = sb("gw16", [P, 2, E], F16)
        gb = sb("gb", [P, E], F32)
        b1_in = sb("b1_in", [E * FC, P], F32)
        b1T = sb("b1T", [P, E * FC], F32)
        b2_in = sb("b2_in", [P, E * D], F32)
        stats = sb("stats", [P, NT, 6], F32)
        mv = sb("mv", [P, NT, 2], F32)
        rs = sb("rs", [P, 4, NT], F32)
        lg = sb("lg", [P, 6, NT, E], F32)
        eidx = sb("eidx", [P, E], F32)
        top = sb("top", [P, 8, NT], F32)
        comb = sb("comb", [P, NT, E], F32)
        h32 = sb("h32", [P, FC, SEQ], F32)
        h_hi = sb("h_hi", [P, FC, SEQ], F16)
        h_lo = sb("h_lo", [P, FC, SEQ], F16)
        q_st = [[sb(f"q_st{s}{h}", [P, SEQ], F16) for h in range(2)] for s in range(SLOTS)]
        k_hi = [sb(f"k_hi{s}", [P, SEQ], F16) for s in range(SLOTS)]
        k_lo = [sb(f"k_lo{s}", [P, SEQ], F16) for s in range(SLOTS)]
        VW = 2 * DH + 2
        v_sp = [sb(f"v_sp{s}", [P, QT, VW], F16) for s in range(SLOTS)]
        nslope_now = sb("nslope_now", [P, SLOTS, 2], F32)
        nmax = sb("nmax", [P, 2, 2], F32)
        h32_16 = h32[:, :, :].rearrange("p a b -> p (a b)").bitcast(F16)
        t_lo = [h32_16[:, i * SEQ:(i + 1) * SEQ] for i in range(NG)]
        rden = sb("rden", [P, SLOTS, 2, QT], F32)
        aT_hi = [h_hi[:, s, :] for s in range(SLOTS)]
        aT_lo = [h_hi[:, SLOTS + s, :] for s in range(SLOTS)]
        flat = stage[:, :, :].rearrange("p a b -> p (a b)")

        def piece(i):
            return flat[:, i * SEQ:(i + 1) * SEQ]

        neg_s = [piece(i) for i in range(2)]
        prob = [piece(2 + i) for i in range(2)]
        t_p = [piece(4 + i) for i in range(NG)]
        a_sb = [piece(9 + s).rearrange("p (t c) -> p t c", t=QT) for s in range(SLOTS)]

        ps = [ctx.enter_context(nc.psum_tensor(f"ps{i}", [P, 512], F32)) for i in range(8)]

        names = """x0 x1 x2 x3 w0 w1 w2 w3 wq0 wq1 wo sm ident consts vec stg small
            stat rstd xn xtr xhi xlo b1tr b1 gate chain comb whi wlo wqkv mixz attz var topexp gap setup rd slope
            hmm gelu hhi hlo ymm yev silu
            S ttr exp T evA evD lo pv nrm ta ah al op acc qmm qh ql kmm kh kl vmm vh vl
            fin outd""".split()
        s = {n: sem("s_" + n) for n in names}

        block = ctx.enter_context(nc.Block())

        def upper(ap):
            return ap.bitcast(BF16).rearrange("p (c two) -> p c two", two=2)[:, :, 1]

        def evA_count(n, u):
            return n * (len(ON_ACT) * SLOTS) + sum(1 for v in range(u) if v % NG in ON_ACT)

        def evD_count(n, u):
            return n * ((NG - len(ON_ACT)) * SLOTS) + sum(1 for v in range(u) if v % NG not in ON_ACT)

        def wait_evicted(eng, n, u):
            if u < 0:
                n, u = n - 1, u + GB
            if u % NG in ON_ACT:
                eng.wait_ge(s["evA"], evA_count(n, u) + 1)
            else:
                eng.wait_ge(s["evD"], evD_count(n, u) + 1)

        def bodies(eng, emit, epilogue):
            emit(0, True)
            with eng.Fori(1, BODIES) as n_:
                emit(n_, False)
            epilogue()

        def evict(n, first, u, eng, on_act):
            v = u - LAG_T
            if first and v < 0:
                return
            m, w = (n, v) if v >= 0 else (n - 1, v + GB)
            if (w % NG in ON_ACT) != on_act:
                return
            eng.wait_ge(s["T"], m * GB + w + 1)
            if not (first and v < NG):
                eng.wait_ge(s["pv"], m * GB + w - NG + 1)
            if on_act:
                eng.copy(t_p[w % NG], ps[2 + w % 2][:, :]).then_inc(s["evA"], 1)
            else:
                eng.tensor_copy(t_p[w % NG], ps[2 + w % 2][:, :]).then_inc(s["evD"], 1)

        def nxt(n):
            return (n + 1) % BODIES

        @block.sync
        def _(sp):
            xt = x.rearrange("b (t p) d -> p (b t) d", p=P)
            for c in range(4):
                sp.dma_start(X[:, 8 * c:8 * c + 8, :], xt[:, 8 * c:8 * c + 8, :]).then_inc(s[f"x{c}"], 16)
            sp.dma_start(gw[:, 0:E], gate_w).then_inc(s["sm"], 16)
            sp.dma_start(gb[:, :], gate_b.rearrange("(a e) -> a e", a=1).to_broadcast([P, E])).then_inc(s["sm"], 16)
            sp.dma_start(b1_in[:, :], b1.rearrange("e (c p) -> (e c) p", p=P)).then_inc(s["sm"], 16)
            for r in (0, 32):
                sp.dma_start(b2_in[r:r + 1, :], b2.rearrange("(a e) d -> a (e d)", a=1)).then_inc(s["sm"], 16)
            w1v = w1.rearrange("e d f -> d e f")
            w2v = w2.rearrange("e (c p) d -> p (e c) d", p=P)
            for c in range(2):
                sp.dma_start(stage[:, 2 * c, :].rearrange("p (e f) -> p e f", f=FF),
                             w1v[:, 4 * c:4 * c + 4, :]).then_inc(s[f"w{2 * c}"], 16)
                sp.dma_start(stage[:, 2 * c + 1, :].rearrange("p (g d) -> p g d", d=D),
                             w2v[:, 16 * c:16 * c + 16, :]).then_inc(s[f"w{2 * c + 1}"], 16)
            for c in range(2):
                sp.wait_ge(s["wlo"], c + 1)
                sp.dma_start(stage[:, c, :], w_qkv[:, c * CH:(c + 1) * CH]).then_inc(s[f"wq{c}"], 16)
            sp.wait_ge(s["wlo"], 3)
            sp.dma_start(stage[:, 2, :].rearrange("p (j d) -> p j d", d=D),
                         w_out.rearrange("(j p) d -> p j d", p=P)).then_inc(s["wo"], 16)
            ot = out.rearrange("b (t p) d -> p (b t) d", p=P)
            for c in range(4):
                sp.wait_ge(s["fin"], c + 1)
                sp.dma_start(ot[:, 8 * c:8 * c + 8, :], X[:, 8 * c:8 * c + 8, :]).then_inc(s["outd"], 16)
            sp.wait_ge(s["outd"], 64)

        @block.gpsimd
        def _(pool):
            pool.memset(ident[:, :], 0.0).then_inc(s["small"], 1)
            pool.iota(eidx[:, :], [[1, E]], base=0, channel_multiplier=0,
                      allow_small_or_imprecise_dtypes=True).then_inc(s["consts"], 1)
            pool.memset(b2_row[:, :, :, :], 0.0).then_inc(s["consts"], 1)
            pool.memset(ones[:, :], 1.0).then_inc(s["consts"], 1)
            pool.wait_ge(s["small"], 1)
            pool.affine_select(out=ident[:, :], in_=ident[:, :], compare_op=ALU.not_equal, fill=1.0,
                               base=0, pattern=[[-1, P]], channel_multiplier=1).then_inc(s["ident"], 1)
            pool.iota(relpos[:, :], [[1, SEQ]], base=-(SEQ - P), channel_multiplier=-1,
                      allow_small_or_imprecise_dtypes=True).then_inc(s["small"], 1)
            pool.wait_ge(s["small"], 2)
            pool.affine_select(out=relpos[:, :], in_=relpos[:, :], compare_op=ALU.is_ge, fill=-BIG,
                               base=SEQ - P, pattern=[[-1, SEQ]], channel_multiplier=1).then_inc(s["consts"], 1)
            for h in range(HQ):
                pool.memset(nslope[:, h:h + 1], -slopes[h])
                pool.memset(qscale[:, h:h + 1], DH ** -0.5 / WS / slopes[h])
            for sl in range(SLOTS):
                pool.memset(v_sp[sl][:, :, DH:DH + 1], 1.0)
            pool.memset(mix[:, :, :], 0.0).then_inc(s["mixz"], 1)

            pool.wait_ge(s["xtr"], NB)
            pool.memset(att[:, :, :], 0.0).then_inc(s["attz"], 1)

            n = 0

            def split(src, hi, lo, scale):
                nonlocal n
                if scale:
                    pool.tensor_scalar(src, src, WS, 1.0, ALU.mult, ALU.mult).then_inc(s["stg"], 1)
                    n += 1
                    pool.wait_ge(s["stg"], n)
                pool.tensor_copy(hi, src).then_inc(s["stg"], 1)
                n += 1
                pool.wait_ge(s["stg"], n)
                pool.tensor_tensor(lo, src, hi, ALU.subtract).then_inc(s["wqkv"], 1)

            pool.wait_ge(s["wq0"], 16)
            split(stage[:, 0, :], wq_hi[:, :], wq_lo[:, :], True)
            pool.wait_ge(s["wq1"], 16)
            ks = stage[:, 1, 0:HKV * DH].rearrange("p (j c) -> p j c", c=DH)
            split(ks, wk_hi[:, :, 0, :], wk_lo[:, :, 0, :], True)
            split(ks, wk_hi[:, :, 1, :], wk_lo[:, :, 1, :], False)
            split(stage[:, 1, HKV * DH:CH], wv_hi[:, :], wv_lo[:, :], True)
            pool.wait_ge(s["wo"], 16)
            split(stage[:, 2, :], wo_hi[:, :, :].rearrange("p j d -> p (j d)"),
                  wo_lo[:, :, :].rearrange("p j d -> p (j d)"), True)

            def lo_groups(n):
                for u in range(GB):
                    r = u % NG
                    if r in ON_ACT:
                        pool.wait_ge(s["evA"], evA_count(n, u) + 1)
                    else:
                        pool.wait_ge(s["evD"], evD_count(n, u) + 1)
                    pool.tensor_tensor(t_lo[r], t_p[r], upper(t_p[r]), ALU.subtract).then_inc(s["lo"], 1)

            with pool.Fori(0, BODIES) as n_:
                lo_groups(n_)

        @block.tensor
        def _(pe):
            def three(dst, a_hi, a_lo, b_hi, b_lo, start=True, stop=True, shared_bank=False):
                pe.matmul(dst, a_hi, b_hi, start=start, stop=False, skip_group_check=shared_bank)
                pe.matmul(dst, a_hi, b_lo, start=False, stop=False, skip_group_check=shared_bank)
                return pe.matmul(dst, a_lo, b_hi, start=False, stop=stop, skip_group_check=shared_bank)

            pe.wait_ge(s["ident"], 1)
            for t in range(NT):
                q = t // QT
                if t % QT == 0 and q >= 4:
                    pe.wait_ge(s["xlo"], q - 3)
                pe.wait_ge(s["xn"], t + 1)
                mm = pe.transpose(ps[q % 4][:, (t % QT) * P:(t % QT + 1) * P], att[:, t, :], ident[:, :])
                if t % QT == QT - 1:
                    mm.then_inc(s["xtr"], 1)
            pe.wait_ge(s["sm"], 80)
            pe.transpose(ps[4][:, 0:E * FC], b1_in[:, :], ident[0:E * FC, 0:E * FC]).then_inc(s["b1tr"], 1)
            pe.wait_ge(s["chain"], 1)
            pe.wait_ge(s["xlo"], NB)
            for t in range(NT):
                d = ps[5][:, t * E:(t + 1) * E]
                tok = slice(t * P, (t + 1) * P)
                pe.matmul(d, xT_hi[:, tok], gw16[:, 0, :], start=True, stop=False)
                pe.matmul(d, xT_hi[:, tok], gw16[:, 1, :], start=False, stop=False)
                pe.matmul(d, xT_lo[:, tok], gw16[:, 1, :], start=False, stop=False)
                mm = pe.matmul(d, xT_lo[:, tok], gw16[:, 0, :], start=False, stop=True)
            mm.then_inc(s["gate"], 1)

            def hidden(n, c):
                cols = bass.ds((n % E) * FF + c * P, P)
                tok = bass.ds((n // E) * SEQ, SEQ)
                three(ps[c][:, :], w1_hi[:, cols], w1_lo[:, cols], xT_hi[:, tok], xT_lo[:, tok])\
                    .then_inc(s["hmm"], 1)

            def down(n, c):
                g = (n % E) * FC + c
                if c == 0:
                    pe.wait_ge(s["yev"], n + 1)
                    pe.matmul(ps[4][:, :], ones[:, :],
                              b2_row[:, bass.ds(n % E, 1), :, :].rearrange("p a t d -> p (a t d)"),
                              start=True, stop=False, skip_group_check=True)
                pe.wait_ge(s["hlo"], (n + 1) * FC + c + 1)
                for t in range(QT):
                    tok = slice(t * P, (t + 1) * P)
                    mm = three(ps[4][:, tok], h_hi[:, c, tok], h_lo[:, c, tok],
                               w2_hi[:, bass.ds(g, 1), :].rearrange("p a d -> p (a d)"),
                               w2_lo[:, bass.ds(g, 1), :].rearrange("p a d -> p (a d)"),
                               start=False, stop=(c == FC - 1 and t == QT - 1), shared_bank=True)
                mm.then_inc(s["ymm"], 1)

            pe.wait_ge(s["wlo"], 4)
            pe.wait_ge(s["b1"], 1)
            pe.wait_ge(s["setup"], 1)
            pe.nop().then_inc(s["ymm"], FC)
            pe.nop().then_inc(s["op"], 1)
            pe.nop().then_inc(s["ta"], 1)
            pe.wait_ge(s["consts"], 4)
            for c in range(FC):
                hidden(0, c)
            with pe.Fori(0, NB * E) as n_:
                for c in range(FC):
                    pe.wait_ge(s["gelu"], n_ * FC + c + 1)
                    hidden((n_ + 1) % (NB * E), c)
                    if c > 0:
                        down(n_, c - 1)
                down(n_, FC - 1)

            S_ps, T_ps, O_ps, G_ps = ps[0:2], ps[2:4], ps[4:6], ps[6:8]

            def heads_q(n, sl):
                w = bass.ds(((n % PAIRS) * SLOTS + sl) * P, P)
                tok = bass.ds((n // PAIRS) * SEQ, SEQ)
                three(G_ps[0][:, :], wq_hi[:, w], wq_lo[:, w], xT_hi[:, tok], xT_lo[:, tok])\
                    .then_inc(s["qmm"], 1)

            def head_k(n, sl):
                j = bass.ds((n % PAIRS) * SLOTS + sl, 1)
                tok = bass.ds((n // PAIRS) * SEQ, SEQ)
                three(G_ps[1][:, :], wk_hi[:, j, :, :].rearrange("p a b c -> p (a b c)"),
                      wk_lo[:, j, :, :].rearrange("p a b c -> p (a b c)"), xT_hi[:, tok], xT_lo[:, tok])\
                    .then_inc(s["kmm"], 1)

            def head_v(n, sl, bank):
                w = bass.ds(((n % PAIRS) * SLOTS + sl) * DH, DH)
                for t in range(QT):
                    tok = bass.ds((n // PAIRS) * SEQ + t * P, P)
                    mm = three(bank[:, t * DH:(t + 1) * DH], xT_hi[:, tok], xT_lo[:, tok],
                               wv_hi[:, w], wv_lo[:, w])
                mm.then_inc(s["vmm"], 1)

            def scores(n, u):
                for h, i, c0 in GROUPS[u % NG]:
                    w = (i + 1) * P
                    q = q_st[u // NG][h][:, i * P:(i + 1) * P]
                    d = S_ps[u % 2][:, c0:c0 + w]
                    pe.matmul(d, q, k_hi[u // NG][:, 0:w], start=True, stop=False)
                    mm = pe.matmul(d, q, k_lo[u // NG][:, 0:w], start=False, stop=True)
                mm.then_inc(s["S"], 1)

            def turn(u):
                for b in range(4):
                    mm = pe.transpose(T_ps[u % 2][:, b * P:(b + 1) * P],
                                      prob[u % 2][:, b * P:(b + 1) * P], ident[:, :])
                mm.then_inc(s["T"], 1)

            def values(u):
                sl, r = u // NG, u % NG
                for h, i, c0 in GROUPS[r]:
                    d = O_ps[h][:, i * (DH + 1):(i + 1) * (DH + 1)]
                    for b in range(i + 1):
                        v = v_sp[sl][:, b, :]
                        c = slice(c0 + b * P, c0 + (b + 1) * P)
                        p_hi = upper(t_p[r])[:, c]
                        pe.matmul(d, p_hi, v[:, 0:DH + 1], start=(b == 0), stop=False)
                        pe.matmul(d[:, 0:DH], p_hi, v[:, DH + 1:2 * DH + 1], start=False, stop=False)
                        mm = pe.matmul(d, t_lo[r][:, c], v[:, 0:DH + 1], start=False, stop=(b == i))
                mm.then_inc(s["pv"], 1)

            def turn_out(sl, bank):
                for t in range(QT):
                    mm = pe.transpose(bank[:, t * P:(t + 1) * P], a_sb[sl][:, t, :], ident[:, :])
                mm.then_inc(s["ta"], 1)

            def project(n, bank):
                for t in range(QT):
                    tok = slice(t * P, (t + 1) * P)
                    for sl in range(SLOTS):
                        j = bass.ds((n % PAIRS) * SLOTS + sl, 1)
                        mm = three(bank[:, tok], aT_hi[sl][:, tok], aT_lo[sl][:, tok],
                                   wo_hi[:, j, :].rearrange("p a d -> p (a d)"),
                                   wo_lo[:, j, :].rearrange("p a d -> p (a d)"),
                                   start=(sl == 0), stop=(sl == SLOTS - 1))
                mm.then_inc(s["op"], 1)

            def emit_t(n, first, u):
                v = u - LAG_T
                if first and v < 0:
                    return
                m, w = (n, v) if v >= 0 else (n - 1, v + GB)
                pe.wait_ge(s["exp"], m * GB + w + 1)
                if not (first and v < 2):
                    wait_evicted(pe, n, v - 2)
                turn(w)

            def emit_pv(n, first, u):
                v = u - LAG_PV
                if first and v < 0:
                    return
                m, w = (n, v) if v >= 0 else (n - 1, v + GB)
                pe.wait_ge(s["lo"], m * GB + w + 1)
                if w % NG == 0:
                    pe.wait_ge(s["vl"], m * SLOTS + w // NG + 1)
                    if not (first and w == 0):
                        pe.wait_ge(s["nrm"], (m * SLOTS + w // NG) * 2 - 1)
                if w % NG == 2 and not (first and w < NG):
                    pe.wait_ge(s["nrm"], (m * SLOTS + w // NG) * 2)
                values(w)

            def step(n, first, u):
                if u % NG == 0:
                    pe.wait_ge(s["kl"], n * SLOTS + u // NG + 1)
                    pe.wait_ge(s["ql"], (n * SLOTS + u // NG) * 2 + 2)
                if not (first and u < 2):
                    pe.wait_ge(s["ttr"], n * GB + u - 1)
                scores(n, u)
                emit_t(n, first, u)
                if u == 0:
                    pe.wait_ge(s["ql"], n * 4 + 2)
                    if not first:
                        pe.wait_ge(s["acc"], n)
                    heads_q(n, 1)
                if u == 1:
                    pe.wait_ge(s["vl"], n * SLOTS + 1)
                    head_k(n, 1)
                if u == 2 and not first:
                    pe.wait_ge(s["nrm"], n * 4 - 2)
                    pe.wait_ge(s["ql"], n * 4 + 4)
                    turn_out(0, G_ps[0])
                if u == 4:
                    pe.wait_ge(s["ql"], n * 4 + 4)
                    if not first:
                        pe.wait_ge(s["al"], n * 2 - 1)
                    head_v(n, 1, G_ps[0])
                if u == 5:
                    pe.wait_ge(s["kl"], n * 2 + 2)
                    if not first:
                        pe.wait_ge(s["nrm"], n * 4)
                        turn_out(1, G_ps[1])
                    pe.wait_ge(s["vl"], n * 2 + 2)
                    heads_q(nxt(n), 0)
                if u == 6:
                    if not first:
                        pe.wait_ge(s["al"], n * 2)
                    head_k(nxt(n), 0)
                if u == 7 and not first:
                    pe.wait_ge(s["ql"], n * 4 + 6)
                    project(n - 1, G_ps[0])
                if u == 9:
                    pe.wait_ge(s["kl"], n * 2 + 3)
                    head_v(nxt(n), 0, G_ps[1])
                emit_pv(n, first, u)

            def emit(n, first):
                for u in range(GB):
                    step(n, first, u)

            def epilogue():
                n = BODIES
                for u in range(LAG_PV):
                    if u < LAG_T:
                        emit_t(n, False, u)
                    if u == 2:
                        pe.wait_ge(s["acc"], n)
                        pe.wait_ge(s["nrm"], n * 4 - 2)
                        turn_out(0, G_ps[0])
                    emit_pv(n, False, u)
                pe.wait_ge(s["nrm"], n * 4)
                pe.wait_ge(s["vl"], n * 2 + 1)
                turn_out(1, G_ps[1])
                pe.wait_ge(s["al"], n * 2)
                project(n - 1, G_ps[0])

            pe.wait_ge(s["wqkv"], 5)
            pe.wait_ge(s["gelu"], NB * E * FC)
            pe.wait_ge(s["yev"], NB * E + 1)
            heads_q(0, 0)
            head_k(0, 0)
            pe.wait_ge(s["ql"], 2)
            pe.wait_ge(s["kl"], 1)
            head_v(0, 0, G_ps[1])
            bodies(pe, emit, epilogue)

        @block.scalar
        def _(act):
            act.wait_ge(s["var"], 1)
            act.activation(rs[:, 1, :], rs[:, 0, :], ACT.Sqrt).then_inc(s["rstd"], 1)
            for q in range(NB):
                act.wait_ge(s["xtr"], q + 1)
                act.copy(xT_hi[:, q * SEQ:(q + 1) * SEQ], ps[q % 4][:, :]).then_inc(s["xhi"], 1)
            for c in range(4):
                act.wait_ge(s[f"w{c}"], 16)
                dst = (w1_hi[:, :] if c % 2 == 0 else w2_hi[:, :, :].rearrange("p g d -> p (g d)"))
                act.activation(dst[:, (c // 2) * CH:(c // 2 + 1) * CH], stage[:, c, :], ACT.Copy,
                               scale=WS).then_inc(s["whi"], 1)
            act.wait_ge(s["b1tr"], 1)
            act.copy(b1T[:, :], ps[4][:, 0:E * FC]).then_inc(s["b1"], 1)
            act.wait_ge(s["gap"], 1)
            act.activation(top[:, 5, :], top[:, 4, :], ACT.Exp).then_inc(s["topexp"], 1)

            act.wait_ge(s["b1"], 1)
            def gelu(n, c):
                act.wait_ge(s["hmm"], n * FC + c + 1)
                b = bass.ds((n % E) * FC + c, 1)
                act.activation(h32[:, c, :], ps[c][:, :], ACT.Gelu, bias=b1T[:, b],
                               scale=1.0 / WS).then_inc(s["gelu"], 1)

            act.preload_act_table(ACT.Gelu)
            with act.Fori(0, NB * E) as n_:
                for c in range(FC):
                    act.wait_ge(s["hlo"], n_ * FC + c + 1)
                    gelu(n_, c)
                for c in range(FC):
                    act.wait_ge(s["gelu"], n_ * FC + c + 1)
                    act.wait_ge(s["ymm"], n_ * FC + c + 1)
                    act.copy(h_hi[:, c, :], h32[:, c, :]).then_inc(s["hhi"], 1)
            act.wait_ge(s["yev"], NB * E + 1)
            act.activation(mix[:, :, :], mix[:, :, :], ACT.Silu).then_inc(s["silu"], 1)

            def q_hi(n, sl):
                act.wait_ge(s["qmm"], n * 2 + sl + 1)
                for h in range(2):
                    rows = slice(64 * h, 64 * h + 64)
                    sc = qscale[rows, bass.ds((n % PAIRS) * 4 + sl * 2 + h, 1)]
                    act.activation(q_st[sl][h][rows, :], ps[6][rows, :], ACT.Copy, scale=sc)\
                       .then_inc(s["qh"], 1)

            def k_hi_(n, sl):
                act.wait_ge(s["kmm"], n * 2 + sl + 1)
                act.activation(k_hi[sl][:, :], ps[7][:, :], ACT.Copy, scale=1.0 / WS).then_inc(s["kh"], 1)

            def v_hi_(n, sl, bank):
                act.wait_ge(s["vmm"], n * 2 + sl + 1)
                act.activation(v_sp[sl][:, :, 0:DH], bank[:, 0:QT * DH].rearrange("p (t c) -> p t c", t=QT),
                               ACT.Copy, scale=1.0 / WS).then_inc(s["vh"], 1)

            def out_hi(k, sl, bank):
                act.wait_ge(s["ta"], k * 2 + sl + 2)
                act.copy(aT_hi[sl], bank[:, :]).then_inc(s["ah"], 1)

            def soft(n, u, first):
                act.wait_ge(s["ttr"], n * GB + u + 1)
                if not (first and u < 2):
                    act.wait_ge(s["T"], n * GB + u - 1)
                g = GROUPS[u % NG]
                for k, (h, i, c0) in enumerate(g):
                    w = (i + 1) * P
                    e = act.activation(prob[u % 2][:, c0:c0 + w], neg_s[u % 2][:, c0:c0 + w], ACT.Exp,
                                       bias=nmax[:, u % 2, k:k + 1], scale=-1.0)
                e.then_inc(s["exp"], 1)

            def emit(n, first):
                for u in range(GB):
                    soft(n, u, first)
                    evict(n, first, u, act, True)
                    if u == 0:
                        if not first:
                            act.wait_ge(s["S"], n * GB)
                        q_hi(n, 1)
                    if u == 1:
                        k_hi_(n, 1)
                    if u == 2 and not first:
                        act.wait_ge(s["op"], n)
                        out_hi(n - 1, 0, ps[6])
                    if u == 4:
                        if not first:
                            act.wait_ge(s["pv"], n * GB)
                        v_hi_(n, 1, ps[6])
                    if u == 5:
                        if not first:
                            out_hi(n - 1, 1, ps[7])
                        act.wait_ge(s["S"], n * GB + NG)
                        q_hi(n + 1, 0)
                    if u == 6:
                        k_hi_(n + 1, 0)
                    if u == 9:
                        act.wait_ge(s["pv"], n * GB + NG)
                        v_hi_(n + 1, 0, ps[7])

            def epilogue():
                n = BODIES
                for u in range(LAG_T):
                    evict(n, False, u, act, True)
                act.wait_ge(s["op"], n)
                out_hi(n - 1, 0, ps[6])
                out_hi(n - 1, 1, ps[7])

            act.wait_ge(s["mixz"], 1)
            q_hi(0, 0)
            k_hi_(0, 0)
            v_hi_(0, 0, ps[7])
            act.preload_act_table(ACT.Exp)
            bodies(act, emit, epilogue)

        @block.vector
        def _(dve):
            nvec = 0

            def small(ins):
                nonlocal nvec
                nvec += 1
                ins.then_inc(s["stat"], 1)
                dve.wait_ge(s["stat"], nvec)

            for t in range(NT):
                if t % 8 == 0:
                    dve.wait_ge(s[f"x{t // 8}"], 16)
                dve.bn_stats(stats[:, t, :], X[:, t, :]).then_inc(s["stat"], 1)
                nvec += 1
            for t in range(NT):
                dve.wait_ge(s["stat"], t + 1)
                ins = dve.bn_aggr(mv[:, t, :], stats[:, t, :])
            small(ins)
            dve.tensor_scalar(rs[:, 0, :], mv[:, :, 1], EPS, None, ALU.add).then_inc(s["var"], 1)
            dve.wait_ge(s["rstd"], 1)
            small(dve.reciprocal(rs[:, 2, :], rs[:, 1, :]))
            small(dve.tensor_tensor(rs[:, 3, :], rs[:, 2, :], rs[:, 2, :], ALU.mult))
            small(dve.tensor_tensor(rs[:, 3, :], rs[:, 3, :], rs[:, 0, :], ALU.mult))
            small(dve.tensor_scalar(rs[:, 3, :], rs[:, 3, :], -0.5, 1.5, ALU.mult, ALU.add))
            small(dve.tensor_tensor(rs[:, 2, :], rs[:, 2, :], rs[:, 3, :], ALU.mult))
            for t in range(NT):
                dve.tensor_scalar(att[:, t, :], X[:, t, :], mv[:, t, 0:1], rs[:, 2, t:t + 1],
                                  ALU.subtract, ALU.mult).then_inc(s["xn"], 1)
            dve.wait_ge(s["sm"], 80)
            small(dve.tensor_scalar(gw[:, E:2 * E], gw[:, 0:E], WS, None, ALU.mult))
            small(dve.tensor_copy(gw16[:, 0, :], gw[:, E:2 * E]))
            dve.tensor_tensor(gw16[:, 1, :], gw[:, E:2 * E], gw16[:, 0, :], ALU.subtract).then_inc(s["chain"], 1)
            dve.wait_ge(s["consts"], 4)
            b2v = b2_in[:, :].rearrange("p (e d) -> p e d", d=D)
            small(dve.tensor_scalar(b2v[0:1], b2v[0:1], WS, None, ALU.mult))
            small(dve.tensor_scalar(b2v[32:33], b2v[32:33], WS, None, ALU.mult))
            for t in range(QT):
                small(dve.tensor_copy(b2_row[0:1, :, t, :], b2v[0:1]))
                small(dve.tensor_copy(b2_row[32:33, :, t, :], b2v[32:33]))
            for t in range(QT):
                ins = dve.tensor_tensor(b2_row[32:33, :, t, :], b2v[32:33], b2_row[32:33, :, t, :], ALU.subtract)
            small(ins)
            for q in range(NB):
                dve.wait_ge(s["xhi"], q + 1)
                cols = slice(q * SEQ, (q + 1) * SEQ)
                dve.tensor_tensor(xT_lo[:, cols], ps[q % 4][:, :], xT_hi[:, cols], ALU.subtract)\
                   .then_inc(s["xlo"], 1)
            dve.wait_ge(s["gate"], 1)
            L, t1, one1, L2, one2, cw = (lg[:, i, :, :] for i in range(6))
            small(dve.scalar_tensor_tensor(out=L, in0=ps[5][:, 0:NT * E].rearrange("p (t e) -> p t e", e=E),
                                           scalar=1.0 / WS, in1=gb[:, :].unsqueeze(1).to_broadcast([P, NT, E]),
                                           op0=ALU.mult, op1=ALU.add))

            def over_e(a):
                return a.unsqueeze(2).to_broadcast([P, NT, E])

            ev = eidx[:, :].unsqueeze(1).to_broadcast([P, NT, E])

            def pick(src, val, idx, hot):
                small(dve.tensor_reduce(val, src, AX_X, ALU.max))
                small(dve.tensor_tensor(t1, src, over_e(val), ALU.is_lt))
                small(dve.scalar_tensor_tensor(out=t1, in0=t1, scalar=float(E), in1=ev, op0=ALU.mult, op1=ALU.add))
                small(dve.tensor_reduce(idx, t1, AX_X, ALU.min))
                small(dve.tensor_tensor(hot, ev, over_e(idx), ALU.is_equal))

            pick(L, top[:, 0, :], top[:, 1, :], one1)
            small(dve.scalar_tensor_tensor(out=L2, in0=one1, scalar=-3e38, in1=L, op0=ALU.mult, op1=ALU.add))
            pick(L2, top[:, 2, :], top[:, 3, :], one2)
            dve.tensor_tensor(top[:, 4, :], top[:, 2, :], top[:, 0, :], ALU.subtract).then_inc(s["gap"], 1)
            dve.wait_ge(s["topexp"], 1)
            small(dve.tensor_scalar(top[:, 6, :], top[:, 5, :], WS, WS, ALU.mult, ALU.add))
            small(dve.reciprocal(top[:, 6, :], top[:, 6, :]))
            small(dve.tensor_tensor(top[:, 7, :], top[:, 6, :], top[:, 5, :], ALU.mult))
            small(dve.tensor_tensor(one1, one1, over_e(top[:, 6, :]), ALU.mult))
            small(dve.tensor_tensor(one2, one2, over_e(top[:, 7, :]), ALU.mult))
            small(dve.tensor_tensor(comb[:, :, :], one1, one2, ALU.add))
            for c in range(4):
                dve.wait_ge(s["whi"], c + 1)
                cols = slice((c // 2) * CH, (c // 2 + 1) * CH)
                hi = (w1_hi[:, :] if c % 2 == 0 else w2_hi[:, :, :].rearrange("p g d -> p (g d)"))[:, cols]
                lo = (w1_lo[:, :] if c % 2 == 0 else w2_lo[:, :, :].rearrange("p g d -> p (g d)"))[:, cols]
                dve.scalar_tensor_tensor(out=lo, in0=stage[:, c, :], scalar=WS, in1=hi, op0=ALU.mult,
                                         op1=ALU.subtract).then_inc(s["wlo"], 1)
            dve.wait_ge(s["mixz"], 1)
            dve.wait_ge(s["wlo"], 4)
            dve.nop().then_inc(s["setup"], 1)
            dve.nop().then_inc(s["hlo"], FC)
            dve.nop().then_inc(s["yev"], 1)
            dve.nop().then_inc(s["acc"], 1)

            with dve.Fori(0, NB * E) as n_:
                for c in range(FC):
                    dve.wait_ge(s["hhi"], n_ * FC + c + 1)
                    dve.tensor_tensor(h_lo[:, c, :], h32[:, c, :], h_hi[:, c, :], ALU.subtract).then_inc(s["hlo"], 1)
                dve.wait_ge(s["ymm"], (n_ + 2) * FC)
                for t in range(QT):
                    m = mix[:, bass.ds((n_ // E) * QT + t, 1), :].rearrange("p a d -> p (a d)")
                    cc = comb[:, bass.ds((n_ // E) * QT + t, 1), bass.ds(n_ % E, 1)].rearrange("p a d -> p (a d)")
                    ins = dve.scalar_tensor_tensor(out=m, in0=ps[4][:, t * P:(t + 1) * P], scalar=cc, in1=m,
                                                   op0=ALU.mult, op1=ALU.add)
                ins.then_inc(s["yev"], 1)

            def head_index(n, sl, h):
                return bass.ds((n % PAIRS) * 4 + sl * 2 + h, 1)

            def shift(n, u, first):
                dve.wait_ge(s["S"], n * GB + u + 1)
                if not (first and u < 2):
                    dve.wait_ge(s["exp"], n * GB + u - 1)
                if u % NG == 0:
                    dve.wait_ge(s["slope"], n * SLOTS + u // NG + 1)
                dve.nop(nofuse=True)
                for k, (h, i, c0) in enumerate(GROUPS[u % NG]):
                    w = (i + 1) * P
                    ins = dve.tensor_tensor_reduce(
                        neg_s[u % 2][:, c0:c0 + w], ps[u % 2][:, c0:c0 + w], relpos[:, SEQ - w:SEQ],
                        nslope_now[:, u // NG, h:h + 1], 3e38, ALU.add, ALU.min,
                        nmax[:, u % 2, k:k + 1])
                ins.then_inc(s["ttr"], 1)

            def slopes_for(n, sl):
                dve.tensor_copy(nslope_now[:, sl, :], nslope[:, bass.ds((n % PAIRS) * 4 + sl * 2, 2)])\
                   .then_inc(s["slope"], 1)

            def q_lo(n, sl, cnt):
                for h in range(2):
                    rows, other = slice(64 * h, 64 * h + 64), slice(64 - 64 * h, 128 - 64 * h)
                    dve.wait_ge(s["qh"], cnt * 2 + h + 1)
                    dve.scalar_tensor_tensor(out=q_st[sl][h][other, :], in0=ps[6][rows, :],
                                             scalar=qscale[rows, head_index(n, sl, h)],
                                             in1=q_st[sl][h][rows, :], op0=ALU.mult, op1=ALU.subtract)\
                       .then_inc(s["ql"], 1)

            def k_lo_(sl, cnt):
                dve.wait_ge(s["kh"], cnt + 1)
                dve.scalar_tensor_tensor(out=k_lo[sl][:, :], in0=ps[7][:, :], scalar=1.0 / WS,
                                         in1=k_hi[sl][:, :], op0=ALU.mult, op1=ALU.subtract)\
                   .then_inc(s["kl"], 1)

            def v_lo_(sl, cnt, bank):
                dve.wait_ge(s["vh"], cnt + 1)
                dve.scalar_tensor_tensor(out=v_sp[sl][:, :, DH + 1:2 * DH + 1],
                                         in0=bank[:, 0:QT * DH].rearrange("p (t c) -> p t c", t=QT),
                                         scalar=1.0 / WS, in1=v_sp[sl][:, :, 0:DH],
                                         op0=ALU.mult, op1=ALU.subtract).then_inc(s["vl"], 1)

            def out_lo(sl, cnt, bank):
                dve.wait_ge(s["ah"], cnt + 1)
                dve.tensor_tensor(aT_lo[sl], bank[:, :], aT_hi[sl], ALU.subtract)\
                   .then_inc(s["al"], 1)

            def normalise(m, sl, h, no_prev):
                last = sl * NG + (2 if h == 0 else 4)
                dve.wait_ge(s["pv"], m * GB + last + 1)
                o = ps[4 + h][:, 0:QT * (DH + 1)].rearrange("p (t c) -> p t c", c=DH + 1)
                dve.reciprocal(rden[:, sl, h, :], o[:, :, DH]).then_inc(s["rd"], 1)
                dve.wait_ge(s["rd"], (m * SLOTS + sl) * 2 + h + 1)
                if h == 0 and not no_prev:
                    dve.wait_ge(s["ta"], m * 2 + sl)
                dve.tensor_tensor(a_sb[sl][:, :, h * DH:(h + 1) * DH], o[:, :, 0:DH],
                                  rden[:, sl, h, :].unsqueeze(2).to_broadcast([P, QT, DH]), ALU.mult)\
                   .then_inc(s["nrm"], 1)

            def accumulate(k):
                dve.wait_ge(s["op"], k + 2)
                a = att[:, bass.ds((k // PAIRS) * QT, QT), :].rearrange("p t d -> p (t d)")
                dve.tensor_tensor(a, ps[6][:, :], a, ALU.add).then_inc(s["acc"], 1)

            def emit(n, first):
                for u in range(GB):
                    shift(n, u, first)
                    evict(n, first, u, dve, False)
                    if u == 0:
                        q_lo(n, 1, n * 2 + 1)
                        slopes_for(n, 1)
                    if u == 1:
                        k_lo_(1, n * 2 + 1)
                    if u == 2 and not first:
                        out_lo(0, n * 2 - 2, ps[6])
                    if u == 4:
                        v_lo_(1, n * 2 + 1, ps[6])
                    if u == 5:
                        if not first:
                            out_lo(1, n * 2 - 1, ps[7])
                        q_lo(nxt(n), 0, n * 2 + 2)
                        slopes_for(nxt(n), 0)
                    if u == 6:
                        k_lo_(0, n * 2 + 2)
                    if u == 7 and not first:
                        accumulate(n - 1)
                    if u == 9:
                        v_lo_(0, n * 2 + 2, ps[7])
                    if u == 2 and not first:
                        normalise(n - 1, 1, 0, False)
                    if u == 4 and not first:
                        normalise(n - 1, 1, 1, False)
                    if u == 7:
                        normalise(n, 0, 0, first)
                    if u == 9:
                        normalise(n, 0, 1, first)

            def epilogue():
                n = BODIES
                for u in range(LAG_T):
                    evict(n, False, u, dve, False)
                out_lo(0, n * 2 - 2, ps[6])
                normalise(n - 1, 1, 0, False)
                normalise(n - 1, 1, 1, False)
                out_lo(1, n * 2 - 1, ps[7])
                accumulate(n - 1)

            dve.wait_ge(s["wqkv"], 5)
            dve.wait_ge(s["attz"], 1)
            q_lo(0, 0, 0)
            slopes_for(0, 0)
            k_lo_(0, 0)
            v_lo_(0, 0, ps[7])
            bodies(dve, emit, epilogue)

            dve.wait_ge(s["silu"], 1)
            dve.wait_ge(s["acc"], BODIES + 1)
            for c in range(4):
                tiles = slice(8 * c, 8 * c + 8)
                a, g, xx = (v[:, tiles, :].rearrange("p t d -> p (t d)") for v in (att, mix, X))
                dve.scalar_tensor_tensor(out=a, in0=a, scalar=1.0 / WS, in1=g, op0=ALU.mult, op1=ALU.mult)\
                   .then_inc(s["rd"], 1)
                dve.wait_ge(s["rd"], BODIES * SLOTS * 2 + c + 1)
                dve.tensor_tensor(xx, xx, a, ALU.add).then_inc(s["fin"], 1)


_INS = ["L0_attn_inputs", "L0_attn_W_qkv", "L0_attn_W_out", "L0_ffn_gate_w", "L0_ffn_gate_b",
        "L0_ffn_w1", "L0_ffn_b1", "L0_ffn_w2", "L0_ffn_b2"]


def kernel(**inputs):
    import numpy as _np
    import concourse.bacc as _bacc
    from concourse import mybir as _mybir
    from concourse.bass_utils import run_bass_kernel_spmd as _run

    nc = _bacc.Bacc("TRN2", target_bir_lowering=False, num_devices=1)
    arrays, args = {}, []
    for name in _INS:
        a = _np.ascontiguousarray(inputs[name])
        arrays[f"in_{name}"] = a
        args.append(nc.dram_tensor(f"in_{name}", a.shape, _mybir.dt.from_np(a.dtype), kind="ExternalInput").ap())
    out = nc.dram_tensor("out_x", (NB, SEQ, D), F32, kind="ExternalOutput").ap()
    build(nc, *args, out)
    r = _run(nc, [arrays], core_ids=[0])
    return r.results[0]["out_x"]
```

```python
from contextlib import ExitStack

import numpy as np

import concourse.bass as bass
from concourse import mybir

F32 = mybir.dt.float32
F16 = mybir.dt.float16
BF16 = mybir.dt.bfloat16
ALU = mybir.AluOpType
ACT = mybir.ActivationFunctionType
AX_X = mybir.AxisListType.X

P = 128
NB, SEQ, D = 8, 512, 128
TOK = NB * SEQ
NT = TOK // P
QT = SEQ // P
E, FF = 8, 512
FC = FF // P
HQ, HKV, DH = 32, 16, 64
WS = 64.0
EPS = 1e-5
BIG = 1e30

GROUPS = [[(0, 3, 0)], [(0, 0, 0), (0, 2, 128)], [(0, 1, 0), (1, 1, 256)], [(1, 3, 0)],
          [(1, 0, 0), (1, 2, 128)]]
NG = len(GROUPS)
SLOTS = 2
GB = SLOTS * NG
BODIES = NB * HKV // SLOTS
PAIRS = HKV // SLOTS
ON_ACT = (0, 1, 2, 3, 4, 5, 6, 7, 9)
G_USERS = [[("Q1", 0), ("A0", -1), ("V1", 0), ("Q0", 1), ("O0", -1)],
           [("K1", 0), ("A1", -1), ("K0", 1), ("V0", 1)]]
ORDER = {
    "PE": [
        ("S0", 0), ("S9", -1), ("T7", -1), ("Q1", 0), ("P5", -1), ("T8", -1), ("S1", 0),
        ("T9", -1), ("P6", -1), ("S2", 0), ("S3", 0), ("P7", -1), ("T0", 0), ("P8", -1),
        ("T1", 0), ("A0", -1), ("P9", -1), ("K1", 0), ("P0", 0), ("S4", 0), ("T3", 0), ("P1", 0),
        ("V1", 0), ("S5", 0), ("A1", -1), ("T2", 0), ("Q0", 1), ("S7", 0), ("S6", 0), ("T4", 0),
        ("K0", 1), ("S8", 0), ("P2", 0), ("P3", 0), ("T6", 0), ("O0", -1), ("T5", 0), ("P4", 0),
        ("V0", 1),
    ],
    "ACT": [
        ("E0", 0), ("X9", -1), ("E1", 0), ("X0", 0), ("X1", 0), ("E3", 0), ("A0", -1), ("K1", 0),
        ("E2", 0), ("X3", 0), ("V1", 0), ("A1", -1), ("E4", 0), ("X2", 0), ("Q0", 1), ("X4", 0),
        ("E6", 0), ("E5", 0), ("K0", 1), ("X6", 0), ("X5", 0), ("E7", 0), ("E8", 0), ("V0", 1),
        ("X7", 0), ("E9", 0), ("Q1", 1),
    ],
    "DVE": [
        ("R0", 0), ("V0", 0), ("X8", -1), ("R1", 0), ("Q1", 0), ("N2", -1), ("R3", 0), ("R2", 0),
        ("N3", -1), ("A0", -1), ("K1", 0), ("R4", 0), ("V1", 0), ("R5", 0), ("A1", -1), ("R6", 0),
        ("Q0", 1), ("N0", 0), ("R7", 0), ("K0", 1), ("R8", 0), ("N1", 0), ("O0", -1), ("R9", 0),
    ],
    "POOL": [
        ("L0", 0), ("L1", 0), ("L3", 0), ("L2", 0), ("L4", 0), ("L6", 0), ("L5", 0), ("L7", 0),
        ("L8", 0), ("L9", 0),
    ],
}


def alibi_slopes():
    base = 2.0 ** (-2.0 ** (-(np.log2(HQ) - 3)))
    return (base ** np.arange(1, HQ + 1, dtype=np.float32)).astype(np.float32)


def build(nc, x, w_qkv, w_out, gate_w, gate_b, w1, b1, w2, b2, out):
    slopes = [float(s) for s in alibi_slopes()]
    ctx = ExitStack()
    with ctx:
        def sb(name, shape, dt):
            return ctx.enter_context(nc.sbuf_tensor(name, shape, dt))

        def sem(name):
            return ctx.enter_context(nc.semaphore(name))

        X = sb("X", [P, NT, D], F32)
        ident = sb("ident", [P, P], F32)
        relpos = sb("relpos", [P, SEQ], F32)
        nslope = sb("nslope", [P, HQ], F32)
        qscale = sb("qscale", [P, HQ], F32)
        xT_hi = sb("xT_hi", [P, TOK], F16)
        xT_lo = sb("xT_lo", [P, TOK], F16)
        w1_hi = sb("w1_hi", [P, E * FF], F16)
        w1_lo = sb("w1_lo", [P, E * FF], F16)
        w2_hi = sb("w2_hi", [P, E * FC, D], F16)
        w2_lo = sb("w2_lo", [P, E * FC, D], F16)
        wq_hi = sb("wq_hi", [P, HQ * DH], F16)
        wq_lo = sb("wq_lo", [P, HQ * DH], F16)
        wk_hi = sb("wk_hi", [P, HKV, 2, DH], F16)
        wk_lo = sb("wk_lo", [P, HKV, 2, DH], F16)
        wv_hi = sb("wv_hi", [P, HKV * DH], F16)
        wv_lo = sb("wv_lo", [P, HKV * DH], F16)
        wo_hi = sb("wo_hi", [P, HKV, D], F16)
        wo_lo = sb("wo_lo", [P, HKV, D], F16)
        mix = sb("mix", [P, NT, D], F32)
        att = sb("att", [P, NT, D], F32)
        b2_row = sb("b2_row", [P, E, QT, D], F16)
        ones = sb("ones", [P, P], F16)
        NSTG, CH = 4, 2048
        stage = sb("stage", [P, NSTG, CH], F32)
        gw = sb("gw", [P, 2 * E], F32)
        gw16 = sb("gw16", [P, 2, E], F16)
        gb = sb("gb", [P, E], F32)
        b1_in = sb("b1_in", [E * FC, P], F32)
        b1T = sb("b1T", [P, E * FC], F32)
        b2_in = sb("b2_in", [P, E * D], F32)
        stats = sb("stats", [P, NT, 6], F32)
        mv = sb("mv", [P, NT, 2], F32)
        rs = sb("rs", [P, 4, NT], F32)
        lg = sb("lg", [P, 6, NT, E], F32)
        eidx = sb("eidx", [P, E], F32)
        top = sb("top", [P, 8, NT], F32)
        comb = sb("comb", [P, NT, E], F32)
        h32 = sb("h32", [P, FC, SEQ], F32)
        h_hi = sb("h_hi", [P, FC, SEQ], F16)
        h_lo = sb("h_lo", [P, FC, SEQ], F16)
        q_st = [[sb(f"q_st{s}{h}", [P, SEQ], F16) for h in range(2)] for s in range(SLOTS)]
        k_hi = [sb(f"k_hi{s}", [P, SEQ], F16) for s in range(SLOTS)]
        k_lo = [sb(f"k_lo{s}", [P, SEQ], F16) for s in range(SLOTS)]
        VW = 2 * DH + 2
        v_sp = [sb(f"v_sp{s}", [P, QT, VW], F16) for s in range(SLOTS)]
        nslope_now = sb("nslope_now", [P, SLOTS, 2], F32)
        nmax = sb("nmax", [P, 2, 2], F32)
        h32_16 = h32[:, :, :].rearrange("p a b -> p (a b)").bitcast(F16)
        t_lo = [h32_16[:, i * SEQ:(i + 1) * SEQ] for i in range(NG)]
        rden = sb("rden", [P, SLOTS, 2, QT], F32)
        aT_hi = [h_hi[:, s, :] for s in range(SLOTS)]
        aT_lo = [h_hi[:, SLOTS + s, :] for s in range(SLOTS)]
        flat = stage[:, :, :].rearrange("p a b -> p (a b)")

        def piece(i):
            return flat[:, i * SEQ:(i + 1) * SEQ]

        neg_s = [piece(i) for i in range(2)]
        prob = [piece(2 + i) for i in range(2)]
        t_p = [piece(4 + i) for i in range(NG)]
        a_sb = [piece(9 + s).rearrange("p (t c) -> p t c", t=QT) for s in range(SLOTS)]

        ps = [ctx.enter_context(nc.psum_tensor(f"ps{i}", [P, 512], F32)) for i in range(8)]

        names = """x0 x1 x2 x3 w0 w1 w2 w3 wq0 wq1 wo sm ident consts vec stg small
            stat rstd xn xtr xhi xlo b1tr b1 gate chain comb whi wlo wqkv mixz attz var topexp gap setup gated rd0 rd1 rd2 rd3
            hmm gelu hhi hlo ymm yev silu
            nrmA0 nrmB0 nrmA1 nrmB1 op acc ta0 ta1 ah0 ah1 al0 al1 slope0 slope1
            qmm0 qmm1 qh0 qh1 ql0 ql1 kmm0 kmm1 kh0 kh1 kl0 kl1 vmm0 vmm1 vh0 vh1 vl0 vl1
            fin outd""".split()
        s = {n: sem("s_" + n) for n in names}
        for step in ("scored", "shifted", "exp", "turned", "out", "lo", "valued"):
            for u in range(GB):
                s[f"{step}{u}"] = sem(f"s_{step}{u}")

        block = ctx.enter_context(nc.Block())

        def upper(ap):
            return ap.bitcast(BF16).rearrange("p (c two) -> p c two", two=2)[:, :, 1]

        def need(eng, name, value):
            if not (isinstance(value, int) and value <= 0):
                eng.wait_ge(s[name], value)

        def group_done(eng, step, n, u):
            need(eng, f"{step}{u % GB}", n + u // GB + 1)

        def slot_done(eng, step, n, sl):
            for u in range(sl * NG, sl * NG + NG):
                group_done(eng, step, n, u)

        def evict(eng, n, u):
            group_done(eng, "turned", n, u)
            group_done(eng, "valued", n, u - NG)
            copy = eng.copy if u in ON_ACT else eng.tensor_copy
            copy(t_p[u % NG], T_ps[u % 2][:, :]).then_inc(s[f"out{u}"], 1)

        def run_bodies(eng, engine_name, tasks):
            order = ORDER[engine_name]

            def window(w):
                for name, off in order:
                    n = w + off
                    if not isinstance(w, int) or 0 <= n < BODIES:
                        tasks[name[0]](n, int(name[1:]))

            for w in (-1, 0, 1):
                window(w)
            with eng.Fori(2, BODIES - 1) as w_:
                window(w_)
            for w in (BODIES - 1, BODIES):
                window(w)

        S_ps, T_ps, O_ps, G_ps = ps[0:2], ps[2:4], ps[4:6], ps[6:8]
        bank_of = {name: G_ps[b] for b, users in enumerate(G_USERS) for name, _ in users}

        def bank_free(n, name):
            users = next(users for users in G_USERS if name in [user for user, _ in users])
            i = [user for user, _ in users].index(name)
            for back in range(1, len(users)):
                user, off = users[i - back]
                body = n + off - users[i][1] - (1 if back > i else 0)
                if isinstance(body, int) and body >= BODIES:
                    continue
                last_reader = {"Q": "ql", "K": "kl", "V": "vl", "A": "al", "O": "acc"}[user[0]]
                need(nc.tensor, last_reader + ("" if user[0] == "O" else user[1]), body + 1)
                return

        def head_index(n, sl, h):
            return bass.ds(pair_index(n) * 4 + sl * 2 + h, 1)

        def pair_index(n):
            return n % PAIRS

        def batch_index(n):
            return n // PAIRS

        @block.sync
        def _(sp):
            xt = x.rearrange("b (t p) d -> p (b t) d", p=P)
            for c in range(4):
                sp.dma_start(X[:, 8 * c:8 * c + 8, :], xt[:, 8 * c:8 * c + 8, :]).then_inc(s[f"x{c}"], 16)
            sp.dma_start(gw[:, 0:E], gate_w).then_inc(s["sm"], 16)
            sp.dma_start(gb[:, :], gate_b.rearrange("(a e) -> a e", a=1).to_broadcast([P, E])).then_inc(s["sm"], 16)
            sp.dma_start(b1_in[:, :], b1.rearrange("e (c p) -> (e c) p", p=P)).then_inc(s["sm"], 16)
            for r in (0, 32):
                sp.dma_start(b2_in[r:r + 1, :], b2.rearrange("(a e) d -> a (e d)", a=1)).then_inc(s["sm"], 16)
            w1v = w1.rearrange("e d f -> d e f")
            w2v = w2.rearrange("e (c p) d -> p (e c) d", p=P)
            for c in range(2):
                sp.dma_start(stage[:, 2 * c, :].rearrange("p (e f) -> p e f", f=FF),
                             w1v[:, 4 * c:4 * c + 4, :]).then_inc(s[f"w{2 * c}"], 16)
                sp.dma_start(stage[:, 2 * c + 1, :].rearrange("p (g d) -> p g d", d=D),
                             w2v[:, 16 * c:16 * c + 16, :]).then_inc(s[f"w{2 * c + 1}"], 16)
            for c in range(2):
                sp.wait_ge(s["wlo"], c + 1)
                sp.dma_start(stage[:, c, :], w_qkv[:, c * CH:(c + 1) * CH]).then_inc(s[f"wq{c}"], 16)
            sp.wait_ge(s["wlo"], 3)
            sp.dma_start(stage[:, 2, :].rearrange("p (j d) -> p j d", d=D),
                         w_out.rearrange("(j p) d -> p j d", p=P)).then_inc(s["wo"], 16)
            ot = out.rearrange("b (t p) d -> p (b t) d", p=P)
            for c in range(4):
                sp.wait_ge(s["fin"], c + 1)
                sp.dma_start(ot[:, 8 * c:8 * c + 8, :], X[:, 8 * c:8 * c + 8, :]).then_inc(s["outd"], 16)
            sp.wait_ge(s["outd"], 64)

        @block.gpsimd
        def _(pool):
            pool.memset(ident[:, :], 0.0).then_inc(s["small"], 1)
            pool.iota(eidx[:, :], [[1, E]], base=0, channel_multiplier=0,
                      allow_small_or_imprecise_dtypes=True).then_inc(s["consts"], 1)
            pool.memset(b2_row[:, :, :, :], 0.0).then_inc(s["consts"], 1)
            pool.memset(ones[:, :], 1.0).then_inc(s["consts"], 1)
            pool.wait_ge(s["small"], 1)
            pool.affine_select(out=ident[:, :], in_=ident[:, :], compare_op=ALU.not_equal, fill=1.0,
                               base=0, pattern=[[-1, P]], channel_multiplier=1).then_inc(s["ident"], 1)
            pool.iota(relpos[:, :], [[1, SEQ]], base=-(SEQ - P), channel_multiplier=-1,
                      allow_small_or_imprecise_dtypes=True).then_inc(s["small"], 1)
            pool.wait_ge(s["small"], 2)
            pool.affine_select(out=relpos[:, :], in_=relpos[:, :], compare_op=ALU.is_ge, fill=-BIG,
                               base=SEQ - P, pattern=[[-1, SEQ]], channel_multiplier=1).then_inc(s["consts"], 1)
            for h in range(HQ):
                pool.memset(nslope[:, h:h + 1], -slopes[h])
                pool.memset(qscale[:, h:h + 1], DH ** -0.5 / WS / slopes[h])
            for sl in range(SLOTS):
                pool.memset(v_sp[sl][:, :, DH:DH + 1], 1.0)
            pool.memset(mix[:, :, :], 0.0).then_inc(s["mixz"], 1)

            pool.wait_ge(s["xtr"], NB)
            pool.memset(att[:, :, :], 0.0).then_inc(s["attz"], 1)

            n = 0

            def split(src, hi, lo, scale):
                nonlocal n
                if scale:
                    pool.tensor_scalar(src, src, WS, 1.0, ALU.mult, ALU.mult).then_inc(s["stg"], 1)
                    n += 1
                    pool.wait_ge(s["stg"], n)
                pool.tensor_copy(hi, src).then_inc(s["stg"], 1)
                n += 1
                pool.wait_ge(s["stg"], n)
                pool.tensor_tensor(lo, src, hi, ALU.subtract).then_inc(s["wqkv"], 1)

            pool.wait_ge(s["wq0"], 16)
            split(stage[:, 0, :], wq_hi[:, :], wq_lo[:, :], True)
            pool.wait_ge(s["wq1"], 16)
            ks = stage[:, 1, 0:HKV * DH].rearrange("p (j c) -> p j c", c=DH)
            split(ks, wk_hi[:, :, 0, :], wk_lo[:, :, 0, :], True)
            split(ks, wk_hi[:, :, 1, :], wk_lo[:, :, 1, :], False)
            split(stage[:, 1, HKV * DH:CH], wv_hi[:, :], wv_lo[:, :], True)
            pool.wait_ge(s["wo"], 16)
            split(stage[:, 2, :], wo_hi[:, :, :].rearrange("p j d -> p (j d)"),
                  wo_lo[:, :, :].rearrange("p j d -> p (j d)"), True)

            def lo_part(n, u):
                group_done(pool, "out", n, u)
                r = u % NG
                pool.tensor_tensor(t_lo[r], t_p[r], upper(t_p[r]), ALU.subtract).then_inc(s[f"lo{u}"], 1)

            run_bodies(pool, "POOL", {"L": lo_part})

        @block.tensor
        def _(pe):
            def three(dst, a_hi, a_lo, b_hi, b_lo, start=True, stop=True, shared_bank=False):
                pe.matmul(dst, a_hi, b_hi, start=start, stop=False, skip_group_check=shared_bank)
                pe.matmul(dst, a_hi, b_lo, start=False, stop=False, skip_group_check=shared_bank)
                return pe.matmul(dst, a_lo, b_hi, start=False, stop=stop, skip_group_check=shared_bank)

            pe.wait_ge(s["ident"], 1)
            for t in range(NT):
                q = t // QT
                if t % QT == 0 and q >= 4:
                    pe.wait_ge(s["xlo"], q - 3)
                pe.wait_ge(s["xn"], t + 1)
                mm = pe.transpose(ps[q % 4][:, (t % QT) * P:(t % QT + 1) * P], att[:, t, :], ident[:, :])
                if t % QT == QT - 1:
                    mm.then_inc(s["xtr"], 1)
            pe.wait_ge(s["sm"], 80)
            pe.transpose(ps[4][:, 0:E * FC], b1_in[:, :], ident[0:E * FC, 0:E * FC]).then_inc(s["b1tr"], 1)
            pe.wait_ge(s["chain"], 1)
            pe.wait_ge(s["xlo"], NB)
            for t in range(NT):
                d = ps[5][:, t * E:(t + 1) * E]
                tok = slice(t * P, (t + 1) * P)
                pe.matmul(d, xT_hi[:, tok], gw16[:, 0, :], start=True, stop=False)
                pe.matmul(d, xT_hi[:, tok], gw16[:, 1, :], start=False, stop=False)
                pe.matmul(d, xT_lo[:, tok], gw16[:, 1, :], start=False, stop=False)
                mm = pe.matmul(d, xT_lo[:, tok], gw16[:, 0, :], start=False, stop=True)
            mm.then_inc(s["gate"], 1)

            def hidden(n, c):
                cols = bass.ds((n % E) * FF + c * P, P)
                tok = bass.ds((n // E) * SEQ, SEQ)
                three(ps[c][:, :], w1_hi[:, cols], w1_lo[:, cols], xT_hi[:, tok], xT_lo[:, tok])\
                    .then_inc(s["hmm"], 1)

            def down(n, c):
                g = (n % E) * FC + c
                if c == 0:
                    pe.wait_ge(s["yev"], n + 1)
                    pe.matmul(ps[4][:, :], ones[:, :],
                              b2_row[:, bass.ds(n % E, 1), :, :].rearrange("p a t d -> p (a t d)"),
                              start=True, stop=False, skip_group_check=True)
                pe.wait_ge(s["hlo"], (n + 1) * FC + c + 1)
                for t in range(QT):
                    tok = slice(t * P, (t + 1) * P)
                    mm = three(ps[4][:, tok], h_hi[:, c, tok], h_lo[:, c, tok],
                               w2_hi[:, bass.ds(g, 1), :].rearrange("p a d -> p (a d)"),
                               w2_lo[:, bass.ds(g, 1), :].rearrange("p a d -> p (a d)"),
                               start=False, stop=(c == FC - 1 and t == QT - 1), shared_bank=True)
                mm.then_inc(s["ymm"], 1)

            pe.wait_ge(s["wlo"], 4)
            pe.wait_ge(s["b1"], 1)
            pe.wait_ge(s["setup"], 1)
            pe.nop().then_inc(s["ymm"], FC)
            pe.wait_ge(s["consts"], 4)
            for c in range(FC):
                hidden(0, c)
            with pe.Fori(0, NB * E) as n_:
                for c in range(FC):
                    pe.wait_ge(s["gelu"], n_ * FC + c + 1)
                    hidden((n_ + 1) % (NB * E), c)
                    if c > 0:
                        down(n_, c - 1)
                down(n_, FC - 1)

            def queries(n, sl):
                bank_free(n, f"Q{sl}")
                w = bass.ds((pair_index(n) * SLOTS + sl) * P, P)
                tok = bass.ds(batch_index(n) * SEQ, SEQ)
                three(bank_of[f"Q{sl}"][:, :], wq_hi[:, w], wq_lo[:, w], xT_hi[:, tok], xT_lo[:, tok])\
                    .then_inc(s[f"qmm{sl}"], 1)

            def keys(n, sl):
                bank_free(n, f"K{sl}")
                j = bass.ds(pair_index(n) * SLOTS + sl, 1)
                tok = bass.ds(batch_index(n) * SEQ, SEQ)
                three(bank_of[f"K{sl}"][:, :], wk_hi[:, j, :, :].rearrange("p a b c -> p (a b c)"),
                      wk_lo[:, j, :, :].rearrange("p a b c -> p (a b c)"), xT_hi[:, tok], xT_lo[:, tok])\
                    .then_inc(s[f"kmm{sl}"], 1)

            def vals(n, sl):
                bank_free(n, f"V{sl}")
                w = bass.ds((pair_index(n) * SLOTS + sl) * DH, DH)
                for t in range(QT):
                    tok = bass.ds(batch_index(n) * SEQ + t * P, P)
                    mm = three(bank_of[f"V{sl}"][:, t * DH:(t + 1) * DH], xT_hi[:, tok], xT_lo[:, tok],
                               wv_hi[:, w], wv_lo[:, w])
                mm.then_inc(s[f"vmm{sl}"], 1)

            def scores(n, u):
                sl = u // NG
                if u % NG == 0:
                    need(pe, f"kl{sl}", n + 1)
                    need(pe, f"ql{sl}", n + 1)
                group_done(pe, "shifted", n, u - 2)
                for h, i, c0 in GROUPS[u % NG]:
                    w = (i + 1) * P
                    q = q_st[sl][h][:, i * P:(i + 1) * P]
                    d = S_ps[u % 2][:, c0:c0 + w]
                    pe.matmul(d, q, k_hi[sl][:, 0:w], start=True, stop=False)
                    mm = pe.matmul(d, q, k_lo[sl][:, 0:w], start=False, stop=True)
                mm.then_inc(s[f"scored{u}"], 1)

            def turn(n, u):
                group_done(pe, "exp", n, u)
                group_done(pe, "out", n, u - 2)
                for b in range(4):
                    mm = pe.transpose(T_ps[u % 2][:, b * P:(b + 1) * P],
                                      prob[u % 2][:, b * P:(b + 1) * P], ident[:, :])
                mm.then_inc(s[f"turned{u}"], 1)

            def values(n, u):
                sl, r = u // NG, u % NG
                group_done(pe, "lo", n, u)
                need(pe, f"vl{sl}", n + 1)
                for head, users in (("A", (0, 1, 2)), ("B", (2, 3, 4))):
                    if r in users:
                        need(pe, f"nrm{head}{1 - sl}", n + sl)
                for h, i, c0 in GROUPS[r]:
                    d = O_ps[h][:, i * (DH + 1):(i + 1) * (DH + 1)]
                    for b in range(i + 1):
                        v = v_sp[sl][:, b, :]
                        c = slice(c0 + b * P, c0 + (b + 1) * P)
                        p_hi = upper(t_p[r])[:, c]
                        pe.matmul(d, p_hi, v[:, 0:DH + 1], start=(b == 0), stop=False)
                        pe.matmul(d[:, 0:DH], p_hi, v[:, DH + 1:2 * DH + 1], start=False, stop=False)
                        mm = pe.matmul(d, t_lo[r][:, c], v[:, 0:DH + 1], start=False, stop=(b == i))
                mm.then_inc(s[f"valued{u}"], 1)

            def turn_out(n, sl):
                need(pe, f"nrmA{sl}", n + 1)
                need(pe, f"nrmB{sl}", n + 1)
                bank_free(n, f"A{sl}")
                for t in range(QT):
                    mm = pe.transpose(bank_of[f"A{sl}"][:, t * P:(t + 1) * P], a_sb[sl][:, t, :], ident[:, :])
                mm.then_inc(s[f"ta{sl}"], 1)

            def project(n, _):
                for sl in range(SLOTS):
                    need(pe, f"al{sl}", n + 1)
                bank_free(n, "O0")
                for t in range(QT):
                    tok = slice(t * P, (t + 1) * P)
                    for sl in range(SLOTS):
                        j = bass.ds(pair_index(n) * SLOTS + sl, 1)
                        mm = three(bank_of["O0"][:, tok], aT_hi[sl][:, tok], aT_lo[sl][:, tok],
                                   wo_hi[:, j, :].rearrange("p a d -> p (a d)"),
                                   wo_lo[:, j, :].rearrange("p a d -> p (a d)"),
                                   start=(sl == 0), stop=(sl == SLOTS - 1))
                mm.then_inc(s["op"], 1)

            pe.wait_ge(s["wqkv"], 5)
            pe.wait_ge(s["gelu"], NB * E * FC)
            pe.wait_ge(s["yev"], NB * E + 1)
            run_bodies(pe, "PE", {"Q": queries, "K": keys, "V": vals, "S": scores, "T": turn,
                                  "P": values, "A": turn_out, "O": project})

        @block.scalar
        def _(act):
            act.wait_ge(s["var"], 1)
            act.activation(rs[:, 1, :], rs[:, 0, :], ACT.Sqrt).then_inc(s["rstd"], 1)
            for q in range(NB):
                act.wait_ge(s["xtr"], q + 1)
                act.copy(xT_hi[:, q * SEQ:(q + 1) * SEQ], ps[q % 4][:, :]).then_inc(s["xhi"], 1)
            for c in range(4):
                act.wait_ge(s[f"w{c}"], 16)
                dst = (w1_hi[:, :] if c % 2 == 0 else w2_hi[:, :, :].rearrange("p g d -> p (g d)"))
                act.activation(dst[:, (c // 2) * CH:(c // 2 + 1) * CH], stage[:, c, :], ACT.Copy,
                               scale=WS).then_inc(s["whi"], 1)
            act.wait_ge(s["b1tr"], 1)
            act.copy(b1T[:, :], ps[4][:, 0:E * FC]).then_inc(s["b1"], 1)
            act.wait_ge(s["gap"], 1)
            act.activation(top[:, 5, :], top[:, 4, :], ACT.Exp).then_inc(s["topexp"], 1)

            act.wait_ge(s["b1"], 1)
            def gelu(n, c):
                act.wait_ge(s["hmm"], n * FC + c + 1)
                b = bass.ds((n % E) * FC + c, 1)
                act.activation(h32[:, c, :], ps[c][:, :], ACT.Gelu, bias=b1T[:, b],
                               scale=1.0 / WS).then_inc(s["gelu"], 1)

            act.preload_act_table(ACT.Gelu)
            with act.Fori(0, NB * E) as n_:
                for c in range(FC):
                    act.wait_ge(s["hlo"], n_ * FC + c + 1)
                    gelu(n_, c)
                    act.wait_ge(s["gelu"], n_ * FC + c + 1)
                    act.wait_ge(s["ymm"], n_ * FC + c + 1)
                    act.copy(h_hi[:, c, :], h32[:, c, :]).then_inc(s["hhi"], 1)
            act.wait_ge(s["yev"], NB * E + 1)
            act.activation(mix[:, :, :], mix[:, :, :], ACT.Silu).then_inc(s["silu"], 1)

            def q_hi(n, sl):
                act.wait_ge(s[f"qmm{sl}"], n + 1)
                slot_done(act, "scored", n - 1, sl)
                for h in range(2):
                    rows = slice(64 * h, 64 * h + 64)
                    ins = act.activation(q_st[sl][h][rows, :], bank_of[f"Q{sl}"][rows, :], ACT.Copy,
                                         scale=qscale[rows, head_index(n, sl, h)])
                ins.then_inc(s[f"qh{sl}"], 1)

            def k_hi_part(n, sl):
                act.wait_ge(s[f"kmm{sl}"], n + 1)
                slot_done(act, "scored", n - 1, sl)
                act.activation(k_hi[sl][:, :], bank_of[f"K{sl}"][:, :], ACT.Copy, scale=1.0 / WS)\
                   .then_inc(s[f"kh{sl}"], 1)

            def v_hi_part(n, sl):
                act.wait_ge(s[f"vmm{sl}"], n + 1)
                slot_done(act, "valued", n - 1, sl)
                act.activation(v_sp[sl][:, :, 0:DH],
                               bank_of[f"V{sl}"][:, 0:QT * DH].rearrange("p (t c) -> p t c", t=QT),
                               ACT.Copy, scale=1.0 / WS).then_inc(s[f"vh{sl}"], 1)

            def out_hi(n, sl):
                act.wait_ge(s[f"ta{sl}"], n + 1)
                need(act, "op", n)
                act.copy(aT_hi[sl], bank_of[f"A{sl}"][:, :]).then_inc(s[f"ah{sl}"], 1)

            def exponentials(n, u):
                group_done(act, "shifted", n, u)
                group_done(act, "turned", n, u - 2)
                for k, (h, i, c0) in enumerate(GROUPS[u % NG]):
                    w = (i + 1) * P
                    e = act.activation(prob[u % 2][:, c0:c0 + w], neg_s[u % 2][:, c0:c0 + w], ACT.Exp,
                                       bias=nmax[:, u % 2, k:k + 1], scale=-1.0)
                e.then_inc(s[f"exp{u}"], 1)

            act.wait_ge(s["mixz"], 1)
            act.preload_act_table(ACT.Exp)
            run_bodies(act, "ACT", {"Q": q_hi, "K": k_hi_part, "V": v_hi_part, "A": out_hi,
                                    "E": exponentials, "X": lambda n, u: evict(act, n, u)})

        @block.vector
        def _(dve):
            nvec = 0

            def small(ins):
                nonlocal nvec
                nvec += 1
                ins.then_inc(s["stat"], 1)
                dve.wait_ge(s["stat"], nvec)

            for t in range(NT):
                if t % 8 == 0:
                    dve.wait_ge(s[f"x{t // 8}"], 16)
                dve.bn_stats(stats[:, t, :], X[:, t, :]).then_inc(s["stat"], 1)
                nvec += 1
            for t in range(NT):
                dve.wait_ge(s["stat"], t + 1)
                ins = dve.bn_aggr(mv[:, t, :], stats[:, t, :])
            small(ins)
            dve.tensor_scalar(rs[:, 0, :], mv[:, :, 1], EPS, None, ALU.add).then_inc(s["var"], 1)
            dve.wait_ge(s["rstd"], 1)
            small(dve.reciprocal(rs[:, 2, :], rs[:, 1, :]))
            small(dve.tensor_tensor(rs[:, 3, :], rs[:, 2, :], rs[:, 2, :], ALU.mult))
            small(dve.tensor_tensor(rs[:, 3, :], rs[:, 3, :], rs[:, 0, :], ALU.mult))
            small(dve.tensor_scalar(rs[:, 3, :], rs[:, 3, :], -0.5, 1.5, ALU.mult, ALU.add))
            small(dve.tensor_tensor(rs[:, 2, :], rs[:, 2, :], rs[:, 3, :], ALU.mult))
            for t in range(NT):
                dve.tensor_scalar(att[:, t, :], X[:, t, :], mv[:, t, 0:1], rs[:, 2, t:t + 1],
                                  ALU.subtract, ALU.mult).then_inc(s["xn"], 1)
            dve.wait_ge(s["sm"], 80)
            small(dve.tensor_scalar(gw[:, E:2 * E], gw[:, 0:E], WS, None, ALU.mult))
            small(dve.tensor_copy(gw16[:, 0, :], gw[:, E:2 * E]))
            dve.tensor_tensor(gw16[:, 1, :], gw[:, E:2 * E], gw16[:, 0, :], ALU.subtract).then_inc(s["chain"], 1)
            dve.wait_ge(s["consts"], 4)
            b2v = b2_in[:, :].rearrange("p (e d) -> p e d", d=D)
            small(dve.tensor_scalar(b2v[0:1], b2v[0:1], WS, None, ALU.mult))
            small(dve.tensor_scalar(b2v[32:33], b2v[32:33], WS, None, ALU.mult))
            for t in range(QT):
                small(dve.tensor_copy(b2_row[0:1, :, t, :], b2v[0:1]))
                small(dve.tensor_copy(b2_row[32:33, :, t, :], b2v[32:33]))
            for t in range(QT):
                ins = dve.tensor_tensor(b2_row[32:33, :, t, :], b2v[32:33], b2_row[32:33, :, t, :], ALU.subtract)
            small(ins)
            for q in range(NB):
                dve.wait_ge(s["xhi"], q + 1)
                cols = slice(q * SEQ, (q + 1) * SEQ)
                dve.tensor_tensor(xT_lo[:, cols], ps[q % 4][:, :], xT_hi[:, cols], ALU.subtract)\
                   .then_inc(s["xlo"], 1)
            dve.wait_ge(s["gate"], 1)
            L, t1, one1, L2, one2, cw = (lg[:, i, :, :] for i in range(6))
            small(dve.scalar_tensor_tensor(out=L, in0=ps[5][:, 0:NT * E].rearrange("p (t e) -> p t e", e=E),
                                           scalar=1.0 / WS, in1=gb[:, :].unsqueeze(1).to_broadcast([P, NT, E]),
                                           op0=ALU.mult, op1=ALU.add))

            def over_e(a):
                return a.unsqueeze(2).to_broadcast([P, NT, E])

            ev = eidx[:, :].unsqueeze(1).to_broadcast([P, NT, E])

            def pick(src, val, idx, hot):
                small(dve.tensor_reduce(val, src, AX_X, ALU.max))
                small(dve.tensor_tensor(t1, src, over_e(val), ALU.is_lt))
                small(dve.scalar_tensor_tensor(out=t1, in0=t1, scalar=float(E), in1=ev, op0=ALU.mult, op1=ALU.add))
                small(dve.tensor_reduce(idx, t1, AX_X, ALU.min))
                small(dve.tensor_tensor(hot, ev, over_e(idx), ALU.is_equal))

            pick(L, top[:, 0, :], top[:, 1, :], one1)
            small(dve.scalar_tensor_tensor(out=L2, in0=one1, scalar=-3e38, in1=L, op0=ALU.mult, op1=ALU.add))
            pick(L2, top[:, 2, :], top[:, 3, :], one2)
            dve.tensor_tensor(top[:, 4, :], top[:, 2, :], top[:, 0, :], ALU.subtract).then_inc(s["gap"], 1)
            dve.wait_ge(s["topexp"], 1)
            small(dve.tensor_scalar(top[:, 6, :], top[:, 5, :], WS, WS, ALU.mult, ALU.add))
            small(dve.reciprocal(top[:, 6, :], top[:, 6, :]))
            small(dve.tensor_tensor(top[:, 7, :], top[:, 6, :], top[:, 5, :], ALU.mult))
            small(dve.tensor_tensor(one1, one1, over_e(top[:, 6, :]), ALU.mult))
            small(dve.tensor_tensor(one2, one2, over_e(top[:, 7, :]), ALU.mult))
            small(dve.tensor_tensor(comb[:, :, :], one1, one2, ALU.add))
            for c in range(4):
                dve.wait_ge(s["whi"], c + 1)
                cols = slice((c // 2) * CH, (c // 2 + 1) * CH)
                hi = (w1_hi[:, :] if c % 2 == 0 else w2_hi[:, :, :].rearrange("p g d -> p (g d)"))[:, cols]
                lo = (w1_lo[:, :] if c % 2 == 0 else w2_lo[:, :, :].rearrange("p g d -> p (g d)"))[:, cols]
                dve.scalar_tensor_tensor(out=lo, in0=stage[:, c, :], scalar=WS, in1=hi, op0=ALU.mult,
                                         op1=ALU.subtract).then_inc(s["wlo"], 1)
            dve.wait_ge(s["mixz"], 1)
            dve.wait_ge(s["wlo"], 4)
            dve.nop().then_inc(s["setup"], 1)
            dve.nop().then_inc(s["hlo"], FC)
            dve.nop().then_inc(s["yev"], 1)

            with dve.Fori(0, NB * E) as n_:
                for c in range(FC):
                    dve.wait_ge(s["hhi"], n_ * FC + c + 1)
                    dve.tensor_tensor(h_lo[:, c, :], h32[:, c, :], h_hi[:, c, :], ALU.subtract).then_inc(s["hlo"], 1)
                dve.wait_ge(s["ymm"], (n_ + 2) * FC)
                for t in range(QT):
                    m = mix[:, bass.ds((n_ // E) * QT + t, 1), :].rearrange("p a d -> p (a d)")
                    cc = comb[:, bass.ds((n_ // E) * QT + t, 1), bass.ds(n_ % E, 1)].rearrange("p a d -> p (a d)")
                    ins = dve.scalar_tensor_tensor(out=m, in0=ps[4][:, t * P:(t + 1) * P], scalar=cc, in1=m,
                                                   op0=ALU.mult, op1=ALU.add)
                ins.then_inc(s["yev"], 1)

            def shift(n, u):
                sl = u // NG
                group_done(dve, "scored", n, u)
                group_done(dve, "exp", n, u - 2)
                need(dve, f"slope{sl}", n + 1)
                dve.nop(nofuse=True)
                for k, (h, i, c0) in enumerate(GROUPS[u % NG]):
                    w = (i + 1) * P
                    ins = dve.tensor_tensor_reduce(
                        neg_s[u % 2][:, c0:c0 + w], S_ps[u % 2][:, c0:c0 + w], relpos[:, SEQ - w:SEQ],
                        nslope_now[:, sl, h:h + 1], 3e38, ALU.add, ALU.min, nmax[:, u % 2, k:k + 1])
                ins.then_inc(s[f"shifted{u}"], 1)

            def q_lo(n, sl):
                dve.wait_ge(s[f"qh{sl}"], n + 1)
                for h in range(2):
                    rows, other = slice(64 * h, 64 * h + 64), slice(64 - 64 * h, 128 - 64 * h)
                    ins = dve.scalar_tensor_tensor(
                        out=q_st[sl][h][other, :], in0=bank_of[f"Q{sl}"][rows, :],
                        scalar=qscale[rows, head_index(n, sl, h)], in1=q_st[sl][h][rows, :],
                        op0=ALU.mult, op1=ALU.subtract)
                ins.then_inc(s[f"ql{sl}"], 1)
                dve.tensor_copy(nslope_now[:, sl, :], nslope[:, bass.ds(pair_index(n) * 4 + sl * 2, 2)])\
                   .then_inc(s[f"slope{sl}"], 1)

            def k_lo_part(n, sl):
                dve.wait_ge(s[f"kh{sl}"], n + 1)
                dve.scalar_tensor_tensor(out=k_lo[sl][:, :], in0=bank_of[f"K{sl}"][:, :], scalar=1.0 / WS,
                                         in1=k_hi[sl][:, :], op0=ALU.mult, op1=ALU.subtract)\
                   .then_inc(s[f"kl{sl}"], 1)

            def v_lo_part(n, sl):
                dve.wait_ge(s[f"vh{sl}"], n + 1)
                dve.scalar_tensor_tensor(
                    out=v_sp[sl][:, :, DH + 1:2 * DH + 1],
                    in0=bank_of[f"V{sl}"][:, 0:QT * DH].rearrange("p (t c) -> p t c", t=QT),
                    scalar=1.0 / WS, in1=v_sp[sl][:, :, 0:DH], op0=ALU.mult, op1=ALU.subtract)\
                   .then_inc(s[f"vl{sl}"], 1)

            def out_lo(n, sl):
                dve.wait_ge(s[f"ah{sl}"], n + 1)
                dve.tensor_tensor(aT_lo[sl], bank_of[f"A{sl}"][:, :], aT_hi[sl], ALU.subtract)\
                   .then_inc(s[f"al{sl}"], 1)

            def normalise(n, head):
                sl, h = divmod(head, 2)
                for r in ((0, 1, 2) if h == 0 else (2, 3, 4)):
                    group_done(dve, "valued", n, sl * NG + r)
                need(dve, f"ta{sl}", n)
                o = O_ps[h][:, 0:QT * (DH + 1)].rearrange("p (t c) -> p t c", c=DH + 1)
                dve.reciprocal(rden[:, sl, h, :], o[:, :, DH]).then_inc(s[f"rd{head}"], 1)
                dve.wait_ge(s[f"rd{head}"], n + 1)
                dve.tensor_tensor(a_sb[sl][:, :, h * DH:(h + 1) * DH], o[:, :, 0:DH],
                                  rden[:, sl, h, :].unsqueeze(2).to_broadcast([P, QT, DH]), ALU.mult)\
                   .then_inc(s[f"nrm{'AB'[h]}{sl}"], 1)

            def accumulate(n, _):
                dve.wait_ge(s["op"], n + 1)
                a = att[:, bass.ds(batch_index(n) * QT, QT), :].rearrange("p t d -> p (t d)")
                dve.tensor_tensor(a, bank_of["O0"][:, :], a, ALU.add).then_inc(s["acc"], 1)

            dve.wait_ge(s["wqkv"], 5)
            dve.wait_ge(s["attz"], 1)
            run_bodies(dve, "DVE", {"R": shift, "Q": q_lo, "K": k_lo_part, "V": v_lo_part, "A": out_lo,
                                    "N": normalise, "O": accumulate,
                                    "X": lambda n, u: evict(dve, n, u)})

            dve.wait_ge(s["silu"], 1)
            dve.wait_ge(s["acc"], BODIES)
            for c in range(4):
                tiles = slice(8 * c, 8 * c + 8)
                a, g, xx = (v[:, tiles, :].rearrange("p t d -> p (t d)") for v in (att, mix, X))
                dve.scalar_tensor_tensor(out=a, in0=a, scalar=1.0 / WS, in1=g, op0=ALU.mult, op1=ALU.mult)\
                   .then_inc(s["gated"], 1)
                dve.wait_ge(s["gated"], c + 1)
                dve.tensor_tensor(xx, xx, a, ALU.add).then_inc(s["fin"], 1)


_INS = ["L0_attn_inputs", "L0_attn_W_qkv", "L0_attn_W_out", "L0_ffn_gate_w", "L0_ffn_gate_b",
        "L0_ffn_w1", "L0_ffn_b1", "L0_ffn_w2", "L0_ffn_b2"]


def kernel(**inputs):
    import numpy as _np
    import concourse.bacc as _bacc
    from concourse import mybir as _mybir
    from concourse.bass_utils import run_bass_kernel_spmd as _run

    nc = _bacc.Bacc("TRN2", target_bir_lowering=False, num_devices=1)
    arrays, args = {}, []
    for name in _INS:
        a = _np.ascontiguousarray(inputs[name])
        arrays[f"in_{name}"] = a
        args.append(nc.dram_tensor(f"in_{name}", a.shape, _mybir.dt.from_np(a.dtype), kind="ExternalInput").ap())
    out = nc.dram_tensor("out_x", (NB, SEQ, D), F32, kind="ExternalOutput").ap()
    build(nc, *args, out)
    r = _run(nc, [arrays], core_ids=[0])
    return r.results[0]["out_x"]
```

```python
from contextlib import ExitStack

import numpy as np

import concourse.bass as bass
from concourse import mybir

F32 = mybir.dt.float32
F16 = mybir.dt.float16
U32 = mybir.dt.uint32
BF16 = mybir.dt.bfloat16
ALU = mybir.AluOpType
ACT = mybir.ActivationFunctionType
AX_X = mybir.AxisListType.X

P = 128
NB, SEQ, D = 8, 512, 128
TOK = NB * SEQ
NT = TOK // P
QT = SEQ // P
E, FF = 8, 512
FC = FF // P
HQ, HKV, DH = 32, 16, 64
WS = 64.0
EPS = 1e-5
BIG = 1e30

GROUPS = [[(0, 3, 0)], [(0, 0, 0), (0, 2, 128)], [(0, 1, 0), (1, 1, 256)], [(1, 3, 0)],
          [(1, 0, 0), (1, 2, 128)]]
NG = len(GROUPS)
SLOTS = 2
GB = SLOTS * NG
BODIES = NB * HKV // SLOTS
HALF = BODIES // 2
BLK = 256
NBLK = (2 * TOK + E * (BLK - 1)) // BLK
NBLK += NBLK % 2
BT = BLK // P
PAIRS = HKV // SLOTS
ON_ACT = (0, 1, 2, 3, 4, 5, 6, 9)
G_USERS = [
    [("Q1", 0), ("A0", -1), ("Q0", 1), ("O0", -1)],
    [("V0", 0), ("A1", -1), ("K0", 1)],
]
ORDER = {
    "PE": [
        ("S0", 0), ("T9", -1), ("A0", -1), ("S1", 0), ("P5", -1), ("P7", -1), ("P6", -1),
        ("S2", 0), ("T0", 0), ("P8", -1), ("P9", -1), ("S3", 0), ("T1", 0), ("Q0", 1), ("S4", 0),
        ("T2", 0), ("S5", 0), ("A1", -1), ("T3", 0), ("S6", 0), ("P0", 0), ("S7", 0), ("P1", 0),
        ("P2", 0), ("T4", 0), ("K0", 1), ("T5", 0), ("O0", -1), ("S8", 0), ("P3", 0), ("P4", 0),
        ("T6", 0), ("S9", 0), ("Q1", 1), ("T7", 0), ("V0", 1), ("T8", 0),
    ],
    "ACT": [
        ("X9", -1), ("A0", -1), ("E0", 0), ("E1", 0), ("X0", 0), ("V0", 0), ("E2", 0), ("X1", 0),
        ("E3", 0), ("X2", 0), ("Q0", 1), ("A1", -1), ("E4", 0), ("X3", 0), ("E5", 0), ("X4", 0),
        ("K0", 1), ("X5", 0), ("E6", 0), ("E7", 0), ("X6", 0), ("E8", 0), ("Q1", 1), ("E9", 0),
        ("W0", 1),
    ],
    "DVE": [
        ("R0", 0), ("R1", 0), ("A0", -1), ("N2", -1), ("R2", 0), ("N3", -1), ("R3", 0), ("V0", 0),
        ("R4", 0), ("R5", 0), ("Q0", 1), ("A1", -1), ("R6", 0), ("N0", 0), ("W0", 0), ("M0", 0),
        ("R7", 0), ("K0", 1), ("O0", -1), ("R8", 0), ("N1", 0), ("M1", 0), ("R9", 0), ("X7", 0),
        ("Q1", 1), ("X8", 0),
    ],
    "POOL": [
        ("L0", 0), ("L1", 0), ("L2", 0), ("L3", 0), ("L4", 0), ("G0", 1), ("L5", 0), ("L6", 0),
        ("L7", 0), ("L8", 0), ("L9", 0), ("G1", 1),
    ],
    "SP": [
        ("W0", 0), ("Q1", 0), ("K1", 0), ("Q0", 1), ("K0", 1),
    ],
}

def alibi_slopes():
    base = 2.0 ** (-2.0 ** (-(np.log2(HQ) - 3)))
    return (base ** np.arange(1, HQ + 1, dtype=np.float32)).astype(np.float32)


def build(nc, x, w_qkv, w_out, gate_w, gate_b, w1, b1, w2, b2, out):
    slopes = [float(s) for s in alibi_slopes()]
    ctx = ExitStack()
    with ctx:
        def sb(name, shape, dt):
            return ctx.enter_context(nc.sbuf_tensor(name, shape, dt))

        def sem(name):
            return ctx.enter_context(nc.semaphore(name))

        X = sb("X", [P, NT, D], F32)
        ident = sb("ident", [P, P], F32)
        relpos = sb("relpos", [P, SEQ], F32)
        nslope = sb("nslope", [P, HQ], F32)
        qscale = sb("qscale", [P, HKV], F32)
        xT_hi = sb("xT_hi", [P, TOK], F16)
        xT_lo = sb("xT_lo", [P, TOK], F16)
        wx_hi = sb("wx_hi", [P, E * FC, 2, D], F16)
        wx_lo = sb("wx_lo", [P, E * FC, 2, D], F16)
        wx_raw = sb("wx_raw", [P, 2, D], F32)
        wq_hi = sb("wq_hi", [P, HQ * DH], F16)
        wq_lo = sb("wq_lo", [P, HQ * DH], F16)
        wk_hi = sb("wk_hi", [P, HKV * DH], F16)
        wk_lo = sb("wk_lo", [P, HKV * DH], F16)
        wv_hi = sb("wv_hi", [P, HKV * DH], F16)
        wv_lo = sb("wv_lo", [P, HKV * DH], F16)
        wo_hi = sb("wo_hi", [P, HKV, D], F16)
        wo_lo = sb("wo_lo", [P, HKV, D], F16)
        mix = sb("mix", [P, NT, D], F32)
        att = sb("att", [P, NT, D], F32)
        b2_row = sb("b2_row", [P, E, BT, D], F16)
        ones = sb("ones", [P, P], F16)
        NSTG, CH = 3, 2048
        stage = sb("stage", [P, NSTG, CH], F32)
        gw = sb("gw", [P, 2 * E], F32)
        gw16 = sb("gw16", [P, 2, E], F16)
        gb = sb("gb", [P, E], F32)
        b1_in = sb("b1_in", [E * FC, P], F32)
        b1T = sb("b1T", [P, E * FC], F32)
        stats = sb("stats", [P, NT, 6], F32)
        mv = sb("mv", [P, NT, 2], F32)
        rs = sb("rs", [P, 4, NT], F32)
        eidx = sb("eidx", [P, E], F32)
        top = sb("top", [P, 8, NT], F32)
        tri32 = sb("tri32", [P, P], F32)
        tri = sb("tri", [P, P], F16)
        chosen = sb("chosen", [P, NT + 1, E], F16)
        steps = sb("steps", [P, E, TOK // BLK], F32)
        ecmp = sb("ecmp", [P, E, E], F32)
        block_no = sb("block_no", [P, NBLK, E], F32)
        per_e = sb("per_e", [P, 4, E], F32)
        slot_f = sb("slot_f", [P, 2, NT], F32)
        slot_of = sb("slot_of", [P, 2, NT], U32)
        blk_f = sb("blk_f", [P, NBLK], F32)
        blk_expert = sb("blk_expert", [1, NBLK], U32)
        row_now = sb("row_now", [P, D], F32)
        slot_now = [sb(f"slot_now{k}", [P, 1], U32) for k in range(2)]
        y_now = [sb(f"y_now{k}", [P, D], F32) for k in range(2)]
        h32 = sb("h32", [P, 2, FC, BLK], F32)
        h_hi = sb("h_hi", [P, 2, FC, BLK], F16)
        h_lo = sb("h_lo", [P, 2, FC, BLK], F16)
        xg = [sb(f"xg{r}", [P, BT * D], F32)[:, :] for r in range(2)]
        y_sb = [sb(f"y_sb{r}", [P, BT * D], F32)[:, :] for r in range(2)]
        xgT_hi = [sb(f"xgT_hi{r}", [P, BLK], F16)[:, :] for r in range(2)]
        xgT_lo = [sb(f"xgT_lo{r}", [P, BLK], F16)[:, :] for r in range(2)]
        h32_flat = h32[:, :, :, :].rearrange("p r a b -> p (r a b)")
        lg = h32_flat[:, 0:6 * NT * E].rearrange("p (i t e) -> p i t e", i=6, e=E)
        scratch = h32_flat[:, 6 * NT * E:6 * NT * E + NBLK * E]
        b2_in = h_lo[:, :, :, :].rearrange("p r a b -> p (r a b)").bitcast(F32)
        q_raw = [sb(f"q_raw{s}", [P, 2, SEQ], F16) for s in range(SLOTS)]
        k_raw = sb("k_raw", [P, 2, SEQ], F16)
        q_st = [[sb(f"q_st{s}{h}", [P, SEQ], F16) for h in range(2)] for s in range(SLOTS)]
        k_st = [sb(f"k_st{s}", [P, 2, SEQ], F16) for s in range(SLOTS)]
        V_HI, V_LO = 2, 4 + SLOTS * DH
        VW = V_LO + SLOTS * DH
        OUT_COL, DEN_COL = (1, 0), (0, DH)
        v_sp = sb("v_sp", [P, QT, VW], F16)
        nslope_now = sb("nslope_now", [P, SLOTS, 2], F32)
        nmax = sb("nmax", [P, 2, 2], F32)
        h32_16 = h32_flat.bitcast(F16)
        t_lo = [h32_16[:, i * SEQ:(i + 1) * SEQ] for i in range(NG)]
        rden = sb("rden", [P, SLOTS, 2, QT], F32)
        h_flat = h_hi[:, :, :, :].rearrange("p r a b -> p (r a b)")
        aT_hi = [h_flat[:, s * SEQ:(s + 1) * SEQ] for s in range(SLOTS)]
        aT_lo = [h_flat[:, (SLOTS + s) * SEQ:(SLOTS + s + 1) * SEQ] for s in range(SLOTS)]
        flat = stage[:, :, :].rearrange("p a b -> p (a b)")

        def piece(i):
            return flat[:, i * SEQ:(i + 1) * SEQ]

        neg_s = [piece(i) for i in range(2)]
        prob = [piece(2 + i) for i in range(2)]
        t_p = [piece(4 + i) for i in range(NG)]
        a_sb = [piece(9 + s).rearrange("p (t c) -> p t c", t=QT) for s in range(SLOTS)]

        slot_x = nc.dram_tensor("slot_x", (NBLK * BLK, D), F32).ap()
        slot_y = nc.dram_tensor("slot_y", (NBLK * BLK, D), F32).ap()

        ps = [ctx.enter_context(nc.psum_tensor(f"ps{i}", [P, 512], F32)) for i in range(8)]

        names = """x0 x1 x2 x3 wq0 wq1 wo sm ident consts small
            stat rstd xn xtr xhi xlo b1tr b1 gate gate_w whi wloD wloP attz var topexp gap silu
            scaled picked ranked routed zeros ready sent got0 got1 added0 added1
            xload0 xload1 w_in w_hi w_lo xturn0 xturn1 gx_hi0 gx_hi1 gx_lo0 gx_lo1 ymm0 ymm1 yout0 yout1 ystore0 ystore1
            hmm00 hmm01 hmm10 hmm11 gelu00 gelu01 gelu10 gelu11 hhi00 hhi01 hhi10 hhi11
            hlo00 hlo01 hlo10 hlo11
            gated rd0 rd1 rd2 rd3 nrmA0 nrmB0 nrmA1 nrmB1 op acc ta0 ta1 ah0 ah1 al0 al1 slope0 slope1
            qst0 qst1 kst0 kst1 scales
            qmm0 qmm1 qh0 qh1 ql0 ql1 kmm kh kl vmm vh vl
            finD finP outd""".split()
        s = {n: sem("s_" + n) for n in names}
        for step in ("scored", "shifted", "exp", "turned", "out", "lo", "valued"):
            for u in range(NG):
                s[f"{step}{u}"] = sem(f"s_{step}{u}")

        block = ctx.enter_context(nc.Block())

        def upper(ap):
            return ap.bitcast(BF16).rearrange("p (c two) -> p c two", two=2)[:, :, 1]

        def need(eng, name, value):
            if not (isinstance(value, int) and value <= 0):
                eng.wait_ge(s[name], value)

        def group_done(eng, step, n, u):
            need(eng, f"{step}{u % NG}", n * SLOTS + u // NG + 1)

        def slot_done(eng, step, n, sl):
            for u in range(sl * NG, sl * NG + NG):
                group_done(eng, step, n, u)

        def evict(eng, n, u):
            group_done(eng, "turned", n, u)
            group_done(eng, "valued", n, u - NG)
            copy = eng.copy if u in ON_ACT else eng.tensor_copy
            copy(t_p[u % NG], T_ps[u % 2][:, :]).then_inc(s[f"out{u % NG}"], 1)

        bodies_of_half = [0, HALF]

        def one_window(engine_name, tasks, w, lo, hi):
            for name, off in ORDER[engine_name]:
                n = w + off
                if name[0] in tasks and (not isinstance(w, int) or lo <= n < hi):
                    tasks[name[0]](n, int(name[1:]))

        def enter_bodies(engine_name, tasks, lo, hi):
            bodies_of_half[:] = lo, hi
            one_window(engine_name, tasks, lo - 1, lo, hi)

        def run_bodies(eng, engine_name, tasks, lo, hi):
            start = max(lo + 1, 2)
            for w in range(lo, start):
                one_window(engine_name, tasks, w, lo, hi)
            with eng.Fori(start, hi - 1) as w_:
                one_window(engine_name, tasks, w_, lo, hi)
            for w in (hi - 1, hi):
                one_window(engine_name, tasks, w, lo, hi)

        stage_of = [stage[:, i, :] for i in range(NSTG)]
        SPLITS = [
            ("wq0", stage_of[0], wq_hi[:, :], wq_lo[:, :]),
            ("wq1", stage_of[1][:, 0:HKV * DH], wk_hi[:, :], wk_lo[:, :]),
            ("wq1", stage_of[1][:, HKV * DH:CH], wv_hi[:, :], wv_lo[:, :]),
            ("wo", stage_of[2], wo_hi[:, :, :].rearrange("p j d -> p (j d)"),
             wo_lo[:, :, :].rearrange("p j d -> p (j d)")),
        ]
        ON_POOL = (2,)
        ON_DVE = tuple(i for i in range(len(SPLITS)) if i not in ON_POOL)
        ZERO_DMAS = -(-NBLK * BT // NT)

        def wx_chunk(w, n):
            return w[:, bass.ds(n, 1), :, :].rearrange("p g a d -> p (g a d)")

        def split_hi(eng, which):
            for i in which:
                name, src, hi, _ = SPLITS[i]
                eng.wait_ge(s[name], 16)
                eng.activation(hi, src, ACT.Copy, scale=WS).then_inc(s["whi"], 1)

        def split_lo(eng, sem_name, which):
            for i in which:
                _, src, hi, lo = SPLITS[i]
                eng.wait_ge(s["whi"], i + 1)
                if eng is nc.gpsimd:
                    eng.tensor_scalar(src, src, WS, 1.0, ALU.mult, ALU.mult).then_inc(s["scaled"], 1)
                    eng.wait_ge(s["scaled"], which.index(i) + 1)
                    eng.tensor_tensor(lo, src, hi, ALU.subtract).then_inc(s[sem_name], 1)
                    continue
                eng.scalar_tensor_tensor(out=lo, in0=src, scalar=WS, in1=hi, op0=ALU.mult,
                                         op1=ALU.subtract).then_inc(s[sem_name], 1)

        def weights_split(eng):
            eng.wait_ge(s["wloD"], len(ON_DVE))
            eng.wait_ge(s["wloP"], len(ON_POOL))

        RANK = E * FC
        S_ps, T_ps, O_ps, G_ps = ps[0:2], ps[2:4], ps[4:6], ps[6:8]
        bank_of = {name: G_ps[b] for b, users in enumerate(G_USERS) for name, _ in users}

        def bank_free(n, name):
            users = next(users for users in G_USERS if name in [user for user, _ in users])
            i = [user for user, _ in users].index(name)
            for back in range(1, len(users)):
                user, off = users[i - back]
                body = n + off - users[i][1] - (1 if back > i else 0)
                if isinstance(body, int) and not bodies_of_half[0] <= body < bodies_of_half[1]:
                    continue
                last_reader = {"Q": "ql", "K": "kl", "V": "vl", "A": "al", "O": "acc"}[user[0]]
                need(nc.tensor, last_reader + ("" if user[0] in "OKV" else user[1]), body + 1)
                return

        def out_chunk(v, c):
            return v[:, 8 * c:8 * c + 8, :].rearrange("p t d -> p (t d)")

        def v_bank():
            return bank_of["V0"][:, :].rearrange("p (t c) -> p t c", t=QT)

        def kv_head(n, sl):
            return bass.ds(pair_index(n) * SLOTS + sl, 1)

        def pair_index(n):
            return n % PAIRS

        def batch_index(n):
            return n // PAIRS

        @block.sync
        def _(sp):
            xt = x.rearrange("b (t p) d -> p (b t) d", p=P)
            for c in range(4):
                sp.dma_start(X[:, 8 * c:8 * c + 8, :], xt[:, 8 * c:8 * c + 8, :]).then_inc(s[f"x{c}"], 16)
            sp.dma_start(gw[:, 0:E], gate_w).then_inc(s["sm"], 16)
            sp.dma_start(gb[:, :], gate_b.rearrange("(a e) -> a e", a=1).to_broadcast([P, E])).then_inc(s["sm"], 16)
            sp.dma_start(b1_in[:, :], b1.rearrange("e (c p) -> (e c) p", p=P)).then_inc(s["sm"], 16)
            for r in (0, 32):
                sp.dma_start(b2_in[r:r + 1, :], b2.rearrange("(a e) d -> a (e d)", a=1)).then_inc(s["sm"], 16)
            for c in range(2):
                sp.dma_start(stage[:, c, :], w_qkv[:, c * CH:(c + 1) * CH]).then_inc(s[f"wq{c}"], 16)
            sp.dma_start(stage[:, 2, :].rearrange("p (j d) -> p j d", d=D),
                         w_out.rearrange("(j p) d -> p j d", p=P)).then_inc(s["wo"], 16)
            sp.wait_ge(s["attz"], 1)
            zx = slot_x.rearrange("(p a) d -> p (a d)", p=P)
            for c in range(0, NBLK * BT, NT):
                k = min(NT, NBLK * BT - c)
                sp.dma_start(zx[:, c * D:(c + k) * D], att[:, 0:k, :].rearrange("p t d -> p (t d)"))\
                  .then_inc(s["zeros"], 16)

            def stack_queries(n, sl):
                sp.wait_ge(s[f"ql{sl}"], n + 1)
                sp.nop(nofuse=True)
                slot_done(sp, "scored", n - 1, sl)
                sp.nop(nofuse=True)
                for h in range(2):
                    raw = q_raw[sl][64 * h:64 * h + 64]
                    for part in range(2):
                        at = 64 * (part ^ h)
                        sp.dma_start(q_st[sl][h][at:at + 64, :], raw[:, part, :]).then_inc(s[f"qst{sl}"], 16)

            def stack_keys(n, sl):
                sp.wait_ge(s["kl"], n + 1)
                sp.nop(nofuse=True)
                slot_done(sp, "scored", n - 1, sl)
                sp.nop(nofuse=True)
                for at in (0, 64):
                    sp.dma_start(k_st[sl][at:at + 64, :, :].rearrange("p a c -> p (a c)"),
                                 k_raw[64 * sl:64 * sl + 64, :, :].rearrange("p a c -> p (a c)"))\
                      .then_inc(s[f"kst{sl}"], 16)

            w2_chunks = w2.rearrange("e (c p) d -> p (e c) d", p=P)

            def load_weights(n, _):
                need(sp, "w_lo", n)
                sp.nop(nofuse=True)
                w1_chunk = w1[bass.ds(n // FC, 1), :, bass.ds(n % FC * P, P)].rearrange("a d f -> d (a f)")
                w2_chunk = w2_chunks[:, bass.ds(n, 1), :].rearrange("p a d -> p (a d)")
                for k, w in enumerate((w1_chunk, w2_chunk)):
                    sp.dma_start(wx_raw[:, k, :], w).then_inc(s["w_in"], 16)

            stacks = {"Q": stack_queries, "K": stack_keys}
            enter_bodies("SP", {**stacks, "W": load_weights}, 0, HALF)
            run_bodies(sp, "SP", {**stacks, "W": load_weights}, 0, HALF)

            def block_rows(m, b):
                return m[bass.ds(b * BLK, BLK), :].rearrange("(p a) d -> p (a d)", p=P)

            def load(b, i, r):
                need(sp, f"xturn{r}", i)
                sp.dma_start(xg[r], block_rows(slot_x, b)).then_inc(s[f"xload{r}"], 16)

            def store(b, i, r):
                sp.wait_ge(s[f"yout{r}"], i + 1)
                sp.dma_start(block_rows(slot_y, b), y_sb[r]).then_inc(s[f"ystore{r}"], 16)

            sp.wait_ge(s["sent"], 2 * NT * 16)
            for b in range(4):
                load(b, b // 2, b % 2)
            with sp.Fori(0, NBLK // 2 - 2) as i_:
                for r in range(2):
                    load(i_ * 2 + 4 + r, i_ + 2, r)
                    store(i_ * 2 + r, i_, r)
            for b in range(NBLK - 4, NBLK):
                if b == NBLK - 2:
                    enter_bodies("SP", stacks, HALF, BODIES)
                store(b, b // 2, b % 2)

            run_bodies(sp, "SP", stacks, HALF, BODIES)

            ot = out.rearrange("b (t p) d -> p (b t) d", p=P)
            for c, name in ((0, "finP"), (2, "finD"), (1, "finP"), (3, "finD")):
                sp.wait_ge(s[name], c % 2 + 1)
                sp.dma_start(ot[:, 8 * c:8 * c + 8, :], X[:, 8 * c:8 * c + 8, :]).then_inc(s["outd"], 16)
            sp.wait_ge(s["outd"], 64)

        @block.gpsimd
        def _(pool):
            pool.memset(ident[:, :], 0.0).then_inc(s["small"], 1)
            pool.iota(eidx[:, :], [[1, E]], base=0, channel_multiplier=0,
                      allow_small_or_imprecise_dtypes=True).then_inc(s["consts"], 1)
            pool.memset(b2_row[:, :, :, :], 0.0).then_inc(s["consts"], 1)
            pool.memset(ones[:, :], 1.0).then_inc(s["consts"], 1)
            pool.wait_ge(s["small"], 1)
            pool.affine_select(out=ident[:, :], in_=ident[:, :], compare_op=ALU.not_equal, fill=1.0,
                               base=0, pattern=[[-1, P]], channel_multiplier=1).then_inc(s["ident"], 1)
            pool.iota(relpos[:, :], [[1, SEQ]], base=-(SEQ - P), channel_multiplier=-1,
                      allow_small_or_imprecise_dtypes=True).then_inc(s["small"], 1)
            pool.wait_ge(s["small"], 2)
            pool.affine_select(out=relpos[:, :], in_=relpos[:, :], compare_op=ALU.is_ge, fill=-BIG,
                               base=SEQ - P, pattern=[[-1, SEQ]], channel_multiplier=1).then_inc(s["consts"], 1)
            for h in range(HQ):
                pool.memset(nslope[:, h:h + 1], -slopes[h])
            for col in (V_HI - 1, V_HI + SLOTS * DH):
                pool.memset(v_sp[:, :, col:col + 1], 1.0)
            pool.memset(chosen[:, NT, :], 0.0).then_inc(s["consts"], 1)
            pool.iota(steps[:, :, :], [[0, E], [BLK, TOK // BLK]], base=0, channel_multiplier=0,
                      allow_small_or_imprecise_dtypes=True).then_inc(s["consts"], 1)
            pool.iota(ecmp[:, :, :], [[1, E], [-1, E]], base=0, channel_multiplier=0,
                      allow_small_or_imprecise_dtypes=True).then_inc(s["consts"], 1)
            pool.iota(block_no[:, :, :], [[1, NBLK], [0, E]], base=0, channel_multiplier=0,
                      allow_small_or_imprecise_dtypes=True).then_inc(s["consts"], 1)
            pool.memset(tri32[:, :], 1.0).then_inc(s["small"], 1)
            pool.wait_ge(s["small"], 3)
            pool.affine_select(out=tri32[:, :], in_=tri32[:, :], compare_op=ALU.is_ge, fill=0.0,
                               base=-1, pattern=[[1, P]], channel_multiplier=-1).then_inc(s["small"], 1)
            pool.wait_ge(s["small"], 4)
            pool.tensor_copy(tri[:, :], tri32[:, :]).then_inc(s["consts"], 1)
            pool.memset(att[:, :, :], 0.0).then_inc(s["attz"], 1)

            pool.wait_ge(s["sm"], 80)
            pool.wait_ge(s["consts"], 9)
            b2v = b2_in[:, :].rearrange("p (e d) -> p e d", d=D)
            done = 4

            def in_turn(ins):
                nonlocal done
                done += 1
                ins.then_inc(s["small"], 1)
                pool.wait_ge(s["small"], done)

            for row in (0, 32):
                v = b2v[row:row + 1]
                in_turn(pool.tensor_scalar(v, v, WS, 1.0, ALU.mult, ALU.mult))
                for t in range(BT):
                    in_turn(pool.tensor_copy(b2_row[row:row + 1, :, t, :], v))
            for t in range(BT):
                lo = b2_row[32:33, :, t, :]
                in_turn(pool.tensor_tensor(lo, b2v[32:33], lo, ALU.subtract))
            split_lo(pool, "wloP", ON_POOL)

            def send(n, k):
                if k == 0:
                    need(pool, "sent", n * 32)
                    pool.tensor_copy(row_now[:, :], mix[:, bass.ds(n, 1), :].rearrange("p a d -> p (a d)"))\
                        .then_inc(s["ready"], 1)
                indices(n, k)
                pool.wait_ge(s["ready"], n * 3 + 2 + k)
                pool.nop(nofuse=True)
                pool.indirect_dma_start(slot_x[:, :], bass.IndirectOffsetOnAxis(ap=slot_now[k][:, 0:1], axis=0),
                                        row_now[:, :], None).then_inc(s["sent"], 16)

            def indices(t, k):
                pool.tensor_copy(slot_now[k][:, :], slot_of[:, k, bass.ds(t, 1)]).then_inc(s["ready"], 1)

            def fetch(n, k):
                t = n - HALF
                need(pool, f"added{k}", t)
                indices(t, k)
                pool.wait_ge(s["ready"], HALF * 3 + t * 2 + 1 + k)
                pool.nop(nofuse=True)
                pool.indirect_dma_start(y_now[k][:, :], None, slot_y[:, :],
                                        bass.IndirectOffsetOnAxis(ap=slot_now[k][:, 0:1], axis=0))\
                    .then_inc(s[f"got{k}"], 16)

            def lo_part(n, u):
                group_done(pool, "out", n, u)
                r = u % NG
                pool.tensor_tensor(t_lo[r], t_p[r], upper(t_p[r]), ALU.subtract).then_inc(s[f"lo{u % NG}"], 1)

            pool.wait_ge(s["routed"], 1)
            pool.wait_ge(s["zeros"], 16 * ZERO_DMAS)
            enter_bodies("POOL", {"L": lo_part, "G": send}, 0, HALF)
            run_bodies(pool, "POOL", {"L": lo_part, "G": send}, 0, HALF)
            for r in range(2):
                pool.wait_ge(s[f"ystore{r}"], NBLK // 2 * 16)
            enter_bodies("POOL", {"L": lo_part, "G": fetch}, HALF, BODIES)
            run_bodies(pool, "POOL", {"L": lo_part, "G": fetch}, HALF, BODIES)
            for c in range(2):
                pool.wait_ge(s["gated"], c + 1)
                xx = out_chunk(X, c)
                pool.tensor_tensor(xx, xx, out_chunk(att, c), ALU.add).then_inc(s["finP"], 1)

        @block.tensor
        def _(pe):
            def three(dst, a_hi, a_lo, b_hi, b_lo, start=True, stop=True, shared_bank=False):
                pe.matmul(dst, a_hi, b_hi, start=start, stop=False, skip_group_check=shared_bank)
                pe.matmul(dst, a_hi, b_lo, start=False, stop=False, skip_group_check=shared_bank)
                return pe.matmul(dst, a_lo, b_hi, start=False, stop=stop, skip_group_check=shared_bank)

            pe.wait_ge(s["ident"], 1)
            for t in range(NT):
                q = t // QT
                if t % QT == 0 and q >= 4:
                    pe.wait_ge(s["xlo"], q - 3)
                pe.wait_ge(s["xn"], t + 1)
                mm = pe.transpose(ps[q % 4][:, (t % QT) * P:(t % QT + 1) * P], mix[:, t, :], ident[:, :])
                if t % QT == QT - 1:
                    mm.then_inc(s["xtr"], 1)
            pe.wait_ge(s["sm"], 80)
            pe.transpose(ps[4][:, 0:E * FC], b1_in[:, :], ident[0:E * FC, 0:E * FC]).then_inc(s["b1tr"], 1)
            pe.wait_ge(s["gate_w"], 1)
            pe.wait_ge(s["xlo"], NB)
            for t in range(NT):
                d = ps[5][:, t * E:(t + 1) * E]
                tok = slice(t * P, (t + 1) * P)
                pe.matmul(d, xT_hi[:, tok], gw16[:, 0, :], start=True, stop=False)
                pe.matmul(d, xT_hi[:, tok], gw16[:, 1, :], start=False, stop=False)
                pe.matmul(d, xT_lo[:, tok], gw16[:, 1, :], start=False, stop=False)
                mm = pe.matmul(d, xT_lo[:, tok], gw16[:, 0, :], start=False, stop=True)
            mm.then_inc(s["gate"], 1)

            def queries(n, sl):
                bank_free(n, f"Q{sl}")
                w = bass.ds((pair_index(n) * SLOTS + sl) * P, P)
                tok = bass.ds(batch_index(n) * SEQ, SEQ)
                three(bank_of[f"Q{sl}"][:, :], wq_hi[:, w], wq_lo[:, w], xT_hi[:, tok], xT_lo[:, tok])\
                    .then_inc(s[f"qmm{sl}"], 1)

            def keys(n, _):
                bank_free(n, "K0")
                w = bass.ds(pair_index(n) * SLOTS * DH, SLOTS * DH)
                tok = bass.ds(batch_index(n) * SEQ, SEQ)
                three(bank_of["K0"][:, :], wk_hi[:, w], wk_lo[:, w], xT_hi[:, tok], xT_lo[:, tok])\
                    .then_inc(s["kmm"], 1)

            def vals(n, _):
                bank_free(n, "V0")
                if isinstance(n, int) and n == 0:
                    pe.wait_ge(s["wloP"], 1)
                w = bass.ds(pair_index(n) * SLOTS * DH, SLOTS * DH)
                tokens = bass.ds(batch_index(n) * SEQ, SEQ)
                x_hi, x_lo = xT_hi[:, tokens], xT_lo[:, tokens]
                for t in range(QT):
                    tok = slice(t * P, (t + 1) * P)
                    mm = three(bank_of["V0"][:, tok], x_hi[:, tok], x_lo[:, tok], wv_hi[:, w], wv_lo[:, w])
                mm.then_inc(s["vmm"], 1)

            def scores(n, u):
                sl = u // NG
                need(pe, f"qst{sl}", (n + 1) * 64)
                need(pe, f"kst{sl}", (n + 1) * 32)
                group_done(pe, "shifted", n, u - 2)
                for h, i, c0 in GROUPS[u % NG]:
                    w = (i + 1) * P
                    q = q_st[sl][h][:, i * P:(i + 1) * P]
                    d = S_ps[u % 2][:, c0:c0 + w]
                    pe.matmul(d, q, k_st[sl][:, 0, 0:w], start=True, stop=False)
                    mm = pe.matmul(d, q, k_st[sl][:, 1, 0:w], start=False, stop=True)
                mm.then_inc(s[f"scored{u % NG}"], 1)

            def turn(n, u):
                group_done(pe, "exp", n, u)
                group_done(pe, "out", n, u - 2)
                for b in range(4):
                    mm = pe.transpose(T_ps[u % 2][:, b * P:(b + 1) * P],
                                      prob[u % 2][:, b * P:(b + 1) * P], ident[:, :])
                mm.then_inc(s[f"turned{u % NG}"], 1)

            def values(n, u):
                sl, r = u // NG, u % NG
                if isinstance(n, int) and n == 0:
                    pe.wait_ge(s["routed"], 1)
                group_done(pe, "lo", n, u)
                need(pe, "vl", n + 1)
                for head, users in (("A", (0, 1, 2)), ("B", (2, 3, 4))):
                    if r in users:
                        need(pe, f"nrm{head}{1 - sl}", n + sl)
                for h, i, c0 in GROUPS[r]:
                    d = O_ps[h][:, i * (DH + 1):(i + 1) * (DH + 1)]
                    with_one = slice(V_HI - 1 + sl * (DH + 1), V_HI - 1 + (sl + 1) * (DH + 1))
                    lo = slice(V_LO + sl * DH, V_LO + (sl + 1) * DH)
                    for b in range(i + 1):
                        v = v_sp[:, b, :]
                        c = slice(c0 + b * P, c0 + (b + 1) * P)
                        p_hi = upper(t_p[r])[:, c]
                        pe.matmul(d, p_hi, v[:, with_one], start=(b == 0), stop=False)
                        pe.matmul(d[:, OUT_COL[sl]:OUT_COL[sl] + DH], p_hi, v[:, lo], start=False, stop=False)
                        mm = pe.matmul(d, t_lo[r][:, c], v[:, with_one], start=False, stop=(b == i))
                mm.then_inc(s[f"valued{u % NG}"], 1)

            def turn_out(n, sl):
                need(pe, f"nrmA{sl}", n + 1)
                need(pe, f"nrmB{sl}", n + 1)
                bank_free(n, f"A{sl}")
                for t in range(QT):
                    mm = pe.transpose(bank_of[f"A{sl}"][:, t * P:(t + 1) * P], a_sb[sl][:, t, :], ident[:, :])
                mm.then_inc(s[f"ta{sl}"], 1)

            def project(n, _):
                for sl in range(SLOTS):
                    need(pe, f"al{sl}", n + 1)
                bank_free(n, "O0")
                for t in range(QT):
                    tok = slice(t * P, (t + 1) * P)
                    for sl in range(SLOTS):
                        j = bass.ds(pair_index(n) * SLOTS + sl, 1)
                        mm = three(bank_of["O0"][:, tok], aT_hi[sl][:, tok], aT_lo[sl][:, tok],
                                   wo_hi[:, j, :].rearrange("p a d -> p (a d)"),
                                   wo_lo[:, j, :].rearrange("p a d -> p (a d)"),
                                   start=(sl == 0), stop=(sl == SLOTS - 1))
                mm.then_inc(s["op"], 1)

            tasks = {"Q": queries, "K": keys, "V": vals, "S": scores, "T": turn, "P": values,
                     "A": turn_out, "O": project}
            pe.wait_ge(s["wloD"], 2)
            enter_bodies("PE", tasks, 0, HALF)

            pe.wait_ge(s["picked"], 1)
            pe.wait_ge(s["b1"], 1)
            rank = ps[4][:, RANK:RANK + (NT + 1) * E]
            pe.matmul(rank, tri[:, :], chosen[:, :, :].rearrange("p t e -> p (t e)"), start=True, stop=False,
                      skip_group_check=True)
            for t in range(NT):
                mm = pe.matmul(rank[:, (t + 1) * E:].rearrange("p (t e) -> p t e", e=E), ones[:, :],
                               chosen[:, t, :].unsqueeze(1).to_broadcast([P, NT - t, E]),
                               start=False, stop=(t == NT - 1), skip_group_check=True)
            mm.then_inc(s["ranked"], 1)

            weights_split(pe)
            run_bodies(pe, "PE", tasks, 0, HALF)

            for u in range(GB):
                group_done(pe, "shifted", HALF - 1, u)
                group_done(pe, "out", HALF - 1, u)
            for sl in range(SLOTS):
                for name in (f"nrmA{sl}", f"nrmB{sl}", f"ql{sl}", f"al{sl}"):
                    pe.wait_ge(s[name], HALF)
            for name in ("kl", "vl", "acc"):
                pe.wait_ge(s[name], HALF)
            pe.wait_ge(s["w_lo"], HALF)

            def turn_rows(i, r):
                pe.wait_ge(s[f"xload{r}"], (i + 1) * 16)
                need(pe, f"gx_lo{r}", i)
                for t in range(BT):
                    mm = pe.transpose(ps[6 + r][:, t * P:(t + 1) * P], xg[r][:, t * P:(t + 1) * P], ident[:, :])
                mm.then_inc(s[f"xturn{r}"], 1)

            def hidden(i, r, e, g):
                if g == 0:
                    pe.wait_ge(s[f"gx_lo{r}"], i + 1)
                need(pe, f"gelu{r}{g}", i)
                for c in (2 * g, 2 * g + 1):
                    w = bass.ds(e * FC + c, 1)
                    mm = three(ps[2 * r + g][:, (c % 2) * BLK:(c % 2 + 1) * BLK],
                               wx_hi[:, w, 0, :].rearrange("p a d -> p (a d)"),
                               wx_lo[:, w, 0, :].rearrange("p a d -> p (a d)"), xgT_hi[r], xgT_lo[r])
                mm.then_inc(s[f"hmm{r}{g}"], 1)

            def down(i, r, e, g):
                y = ps[4 + r]
                if g == 0:
                    need(pe, f"yout{r}", i)
                    pe.matmul(y[:, 0:BLK], ones[:, :], b2_row[:, bass.ds(e, 1), :, :].rearrange("p a t d -> p (a t d)"),
                              start=True, stop=False, skip_group_check=True)
                pe.wait_ge(s[f"hlo{r}{g}"], i + 1)
                for c in (2 * g, 2 * g + 1):
                    w = bass.ds(e * FC + c, 1)
                    for t in range(BT):
                        tok = slice(t * P, (t + 1) * P)
                        mm = three(y[:, tok], h_hi[:, r, c, tok], h_lo[:, r, c, tok],
                                   wx_hi[:, w, 1, :].rearrange("p a d -> p (a d)"),
                                   wx_lo[:, w, 1, :].rearrange("p a d -> p (a d)"),
                                   start=False, stop=(c == FC - 1 and t == BT - 1), shared_bank=True)
                if g == 1:
                    mm.then_inc(s[f"ymm{r}"], 1)

            expert = [pe.alloc_register(f"pe_expert{r}") for r in range(2)]

            def steps_of(i, last):
                e = [pe.snap(reg, min_val=0, max_val=E - 1) for reg in expert]
                for r in range(2):
                    if not last:
                        turn_rows(i + 1, r)
                    for g in range(2):
                        if r == 0 or not last:
                            hidden(i + r, 1 - r, e[r + 1], g)
                        down(i, r, e[r], g)
                        if g == 0 and not last:
                            pe.reg_load(expert[r], blk_expert[0:1, bass.ds(i * 2 + 2 + r, 1)])
                            e.append(pe.snap(expert[r], min_val=0, max_val=E - 1))

            for r in range(2):
                turn_rows(0, r)
                pe.reg_load(expert[r], blk_expert[0:1, r:r + 1])
            e0 = pe.snap(expert[0], min_val=0, max_val=E - 1)
            for g in range(2):
                hidden(0, 0, e0, g)
            steps_of(0, False)
            with pe.Fori(1, NBLK // 2 - 1) as i_:
                steps_of(i_, False)
            pe.wait_ge(s["gx_lo1"], NBLK // 2)
            enter_bodies("PE", tasks, HALF, BODIES)
            steps_of(NBLK // 2 - 1, True)

            for r in range(2):
                pe.wait_ge(s[f"yout{r}"], NBLK // 2)
            run_bodies(pe, "PE", tasks, HALF, BODIES)

        @block.scalar
        def _(act):
            act.wait_ge(s["var"], 1)
            act.activation(rs[:, 1, :], rs[:, 0, :], ACT.Sqrt).then_inc(s["rstd"], 1)
            for q in range(NB):
                act.wait_ge(s["xtr"], q + 1)
                act.copy(xT_hi[:, q * SEQ:(q + 1) * SEQ], ps[q % 4][:, :]).then_inc(s["xhi"], 1)
            split_hi(act, range(len(SPLITS)))
            act.wait_ge(s["b1tr"], 1)
            act.copy(b1T[:, :], ps[4][:, 0:E * FC]).then_inc(s["b1"], 1)
            act.wait_ge(s["gap"], 1)
            act.activation(top[:, 5, :], top[:, 4, :], ACT.Exp).then_inc(s["topexp"], 1)

            def q_hi(n, sl):
                act.wait_ge(s[f"qmm{sl}"], n + 1)
                need(act, f"qst{sl}", n * 64)
                act.activation(q_raw[sl][:, 0, :], bank_of[f"Q{sl}"][:, :], ACT.Copy,
                               scale=qscale[:, kv_head(n, sl)]).then_inc(s[f"qh{sl}"], 1)

            def k_hi_part(n, _):
                act.wait_ge(s["kmm"], n + 1)
                for sl in range(SLOTS):
                    need(act, f"kst{sl}", n * 32)
                act.activation(k_raw[:, 0, :], bank_of["K0"][:, :], ACT.Copy, scale=1.0 / WS)\
                   .then_inc(s["kh"], 1)

            def v_hi_part(n, _):
                act.wait_ge(s["vmm"], n + 1)
                slot_done(act, "valued", n - 1, SLOTS - 1)
                act.activation(v_sp[:, :, V_HI:V_HI + SLOTS * DH], v_bank(),
                               ACT.Copy, scale=1.0 / WS).then_inc(s["vh"], 1)

            def out_hi(n, sl):
                act.wait_ge(s[f"ta{sl}"], n + 1)
                need(act, "op", n)
                act.copy(aT_hi[sl], bank_of[f"A{sl}"][:, :]).then_inc(s[f"ah{sl}"], 1)

            def exponentials(n, u):
                group_done(act, "shifted", n, u)
                group_done(act, "turned", n, u - 2)
                for k, (h, i, c0) in enumerate(GROUPS[u % NG]):
                    w = (i + 1) * P
                    e = act.activation(prob[u % 2][:, c0:c0 + w], neg_s[u % 2][:, c0:c0 + w], ACT.Exp,
                                       bias=nmax[:, u % 2, k:k + 1], scale=-1.0)
                e.then_inc(s[f"exp{u % NG}"], 1)

            def weights_hi(n, _):
                act.wait_ge(s["w_in"], (n + 1) * 32)
                act.activation(wx_chunk(wx_hi, n), wx_raw[:, :, :].rearrange("p a d -> p (a d)"), ACT.Copy,
                               scale=WS).then_inc(s["w_hi"], 1)

            tasks = {"Q": q_hi, "K": k_hi_part, "V": v_hi_part, "A": out_hi, "E": exponentials,
                     "X": lambda n, u: evict(act, n, u)}
            act.wait_ge(s["scales"], HQ)
            enter_bodies("ACT", {**tasks, "W": weights_hi}, 0, HALF)
            weights_split(act)
            act.preload_act_table(ACT.Exp)
            run_bodies(act, "ACT", {**tasks, "W": weights_hi}, 0, HALF)

            def inputs_hi(i, r):
                act.wait_ge(s[f"xturn{r}"], i + 1)
                need(act, f"hmm{r}1", i)
                act.copy(xgT_hi[r], ps[6 + r][:, 0:BLK]).then_inc(s[f"gx_hi{r}"], 1)

            def gelus(i, r, e, g):
                act.wait_ge(s[f"hmm{r}{g}"], i + 1)
                need(act, f"hlo{r}{g}", i)
                for c in (2 * g, 2 * g + 1):
                    ins = act.activation(h32[:, r, c, :], ps[2 * r + g][:, (c % 2) * BLK:(c % 2 + 1) * BLK],
                                         ACT.Gelu, bias=b1T[:, bass.ds(e * FC + c, 1)], scale=1.0 / WS)
                ins.then_inc(s[f"gelu{r}{g}"], 1)

            def expert_of(b):
                return act.value_load(blk_expert[0:1, bass.ds(b, 1)], min_val=0, max_val=E - 1)

            act.preload_act_table(ACT.Gelu)
            for r in range(2):
                inputs_hi(0, r)
            e0 = expert_of(0)
            for g in range(2):
                gelus(0, 0, e0, g)

            def steps_of(i):
                e = [expert_of(i * 2 + 1 + k) for k in range(2)]
                for r in range(2):
                    inputs_hi(i + 1, r)
                    for g in range(2):
                        gelus(i + r, 1 - r, e[r], g)

            steps_of(0)
            with act.Fori(1, NBLK // 2 - 1) as i_:
                steps_of(i_)
            enter_bodies("ACT", tasks, HALF, BODIES)
            e1 = expert_of(NBLK - 1)
            for g in range(2):
                gelus(NBLK // 2 - 1, 1, e1, g)

            act.preload_act_table(ACT.Exp)
            run_bodies(act, "ACT", tasks, HALF, BODIES)
            act.wait_ge(s["added1"], NT)
            act.activation(mix[:, :, :], mix[:, :, :], ACT.Silu).then_inc(s["silu"], 1)

        @block.vector
        def _(dve):
            nvec = 0

            def small(ins):
                nonlocal nvec
                nvec += 1
                ins.then_inc(s["stat"], 1)
                dve.wait_ge(s["stat"], nvec)

            for h in range(HQ):
                rows = slice(64 * (h % 2), 64 * (h % 2) + 64)
                dve.memset(qscale[rows, h // 2:h // 2 + 1], DH ** -0.5 / WS / slopes[h]).then_inc(s["scales"], 1)
            for t in range(NT):
                if t % 8 == 0:
                    dve.wait_ge(s[f"x{t // 8}"], 16)
                dve.bn_stats(stats[:, t, :], X[:, t, :]).then_inc(s["stat"], 1)
                nvec += 1
            for t in range(NT):
                dve.wait_ge(s["stat"], t + 1)
                ins = dve.bn_aggr(mv[:, t, :], stats[:, t, :])
            small(ins)
            dve.tensor_scalar(rs[:, 0, :], mv[:, :, 1], EPS, None, ALU.add).then_inc(s["var"], 1)
            dve.wait_ge(s["rstd"], 1)
            small(dve.reciprocal(rs[:, 2, :], rs[:, 1, :]))
            small(dve.tensor_tensor(rs[:, 3, :], rs[:, 2, :], rs[:, 2, :], ALU.mult))
            small(dve.tensor_tensor(rs[:, 3, :], rs[:, 3, :], rs[:, 0, :], ALU.mult))
            small(dve.tensor_scalar(rs[:, 3, :], rs[:, 3, :], -0.5, 1.5, ALU.mult, ALU.add))
            small(dve.tensor_tensor(rs[:, 2, :], rs[:, 2, :], rs[:, 3, :], ALU.mult))
            for t in range(NT):
                dve.tensor_scalar(mix[:, t, :], X[:, t, :], mv[:, t, 0:1], rs[:, 2, t:t + 1],
                                  ALU.subtract, ALU.mult).then_inc(s["xn"], 1)
            dve.wait_ge(s["sm"], 80)
            small(dve.tensor_scalar(gw[:, E:2 * E], gw[:, 0:E], WS, None, ALU.mult))
            small(dve.tensor_copy(gw16[:, 0, :], gw[:, E:2 * E]))
            dve.tensor_tensor(gw16[:, 1, :], gw[:, E:2 * E], gw16[:, 0, :], ALU.subtract).then_inc(s["gate_w"], 1)
            for q in range(NB):
                dve.wait_ge(s["xhi"], q + 1)
                cols = slice(q * SEQ, (q + 1) * SEQ)
                dve.tensor_tensor(xT_lo[:, cols], ps[q % 4][:, :], xT_hi[:, cols], ALU.subtract)\
                   .then_inc(s["xlo"], 1)
            split_lo(dve, "wloD", ON_DVE[:2])
            dve.wait_ge(s["consts"], 9)
            dve.wait_ge(s["gate"], 1)
            L, t1, one1, L2, one2, cw = (lg[:, i, :, :] for i in range(6))
            small(dve.scalar_tensor_tensor(out=L, in0=ps[5][:, 0:NT * E].rearrange("p (t e) -> p t e", e=E),
                                           scalar=1.0 / WS, in1=gb[:, :].unsqueeze(1).to_broadcast([P, NT, E]),
                                           op0=ALU.mult, op1=ALU.add))

            def over_e(a):
                return a.unsqueeze(2).to_broadcast([P, NT, E])

            ev = eidx[:, :].unsqueeze(1).to_broadcast([P, NT, E])

            def pick(src, val, idx, hot):
                small(dve.tensor_reduce(val, src, AX_X, ALU.max))
                small(dve.tensor_tensor(t1, src, over_e(val), ALU.is_lt))
                small(dve.scalar_tensor_tensor(out=t1, in0=t1, scalar=float(E), in1=ev, op0=ALU.mult, op1=ALU.add))
                small(dve.tensor_reduce(idx, t1, AX_X, ALU.min))
                small(dve.tensor_tensor(hot, ev, over_e(idx), ALU.is_equal))

            pick(L, top[:, 0, :], top[:, 1, :], one1)
            small(dve.scalar_tensor_tensor(out=L2, in0=one1, scalar=-3e38, in1=L, op0=ALU.mult, op1=ALU.add))
            pick(L2, top[:, 2, :], top[:, 3, :], one2)
            dve.tensor_tensor(top[:, 4, :], top[:, 2, :], top[:, 0, :], ALU.subtract).then_inc(s["gap"], 1)
            dve.tensor_tensor(chosen[:, 0:NT, :], one1, one2, ALU.add).then_inc(s["picked"], 1)
            dve.wait_ge(s["topexp"], 1)
            small(dve.tensor_scalar(top[:, 6, :], top[:, 5, :], WS, WS, ALU.mult, ALU.add))
            small(dve.reciprocal(top[:, 6, :], top[:, 6, :]))
            small(dve.tensor_tensor(top[:, 7, :], top[:, 6, :], top[:, 5, :], ALU.mult))
            def shift(n, u):
                sl = u // NG
                group_done(dve, "scored", n, u)
                group_done(dve, "exp", n, u - 2)
                need(dve, f"slope{sl}", n + 1)
                dve.nop(nofuse=True)
                for k, (h, i, c0) in enumerate(GROUPS[u % NG]):
                    w = (i + 1) * P
                    ins = dve.tensor_tensor_reduce(
                        neg_s[u % 2][:, c0:c0 + w], S_ps[u % 2][:, c0:c0 + w], relpos[:, SEQ - w:SEQ],
                        nslope_now[:, sl, h:h + 1], 3e38, ALU.add, ALU.min, nmax[:, u % 2, k:k + 1])
                ins.then_inc(s[f"shifted{u % NG}"], 1)

            def q_lo(n, sl):
                dve.wait_ge(s[f"qh{sl}"], n + 1)
                dve.scalar_tensor_tensor(
                    out=q_raw[sl][:, 1, :], in0=bank_of[f"Q{sl}"][:, :], scalar=qscale[:, kv_head(n, sl)],
                    in1=q_raw[sl][:, 0, :], op0=ALU.mult, op1=ALU.subtract).then_inc(s[f"ql{sl}"], 1)
                slot_done(dve, "shifted", n - 1, sl)
                dve.tensor_copy(nslope_now[:, sl, :], nslope[:, bass.ds(pair_index(n) * 4 + sl * 2, 2)])\
                   .then_inc(s[f"slope{sl}"], 1)

            def k_lo_part(n, _):
                dve.wait_ge(s["kh"], n + 1)
                dve.scalar_tensor_tensor(out=k_raw[:, 1, :], in0=bank_of["K0"][:, :], scalar=1.0 / WS,
                                         in1=k_raw[:, 0, :], op0=ALU.mult, op1=ALU.subtract)\
                   .then_inc(s["kl"], 1)

            def v_lo_part(n, _):
                dve.wait_ge(s["vh"], n + 1)
                dve.scalar_tensor_tensor(
                    out=v_sp[:, :, V_LO:VW], in0=v_bank(),
                    scalar=1.0 / WS, in1=v_sp[:, :, V_HI:V_HI + SLOTS * DH],
                    op0=ALU.mult, op1=ALU.subtract).then_inc(s["vl"], 1)

            def out_lo(n, sl):
                dve.wait_ge(s[f"ah{sl}"], n + 1)
                dve.tensor_tensor(aT_lo[sl], bank_of[f"A{sl}"][:, :], aT_hi[sl], ALU.subtract)\
                   .then_inc(s[f"al{sl}"], 1)

            def normalise(n, head):
                sl, h = divmod(head, 2)
                for r in ((0, 1, 2) if h == 0 else (2, 3, 4)):
                    group_done(dve, "valued", n, sl * NG + r)
                need(dve, f"ta{sl}", n)
                o = O_ps[h][:, 0:QT * (DH + 1)].rearrange("p (t c) -> p t c", c=DH + 1)
                dve.reciprocal(rden[:, sl, h, :], o[:, :, DEN_COL[sl]]).then_inc(s[f"rd{head}"], 1)
                dve.wait_ge(s[f"rd{head}"], n + 1)
                dve.tensor_tensor(a_sb[sl][:, :, h * DH:(h + 1) * DH],
                                  o[:, :, OUT_COL[sl]:OUT_COL[sl] + DH],
                                  rden[:, sl, h, :].unsqueeze(2).to_broadcast([P, QT, DH]), ALU.mult)\
                   .then_inc(s[f"nrm{'AB'[h]}{sl}"], 1)

            def accumulate(n, _):
                dve.wait_ge(s["op"], n + 1)
                a = att[:, bass.ds(batch_index(n) * QT, QT), :].rearrange("p t d -> p (t d)")
                dve.tensor_tensor(a, bank_of["O0"][:, :], a, ALU.add).then_inc(s["acc"], 1)

            def add_expert(n, k):
                t = n - HALF
                dve.wait_ge(s[f"got{k}"], (t + 1) * 16)
                m = mix[:, bass.ds(t, 1), :].rearrange("p a d -> p (a d)")
                weight = top[:, 6 + k, bass.ds(t, 1)]
                if k == 0:
                    ins = dve.tensor_scalar(m, y_now[0][:, :], weight, None, ALU.mult)
                else:
                    dve.wait_ge(s["added0"], t + 1)
                    ins = dve.scalar_tensor_tensor(out=m, in0=y_now[1][:, :], scalar=weight, in1=m,
                                                   op0=ALU.mult, op1=ALU.add)
                ins.then_inc(s[f"added{k}"], 1)

            def weights_lo(n, _):
                dve.wait_ge(s["w_hi"], n + 1)
                dve.scalar_tensor_tensor(out=wx_chunk(wx_lo, n), in0=wx_raw[:, :, :].rearrange("p a d -> p (a d)"),
                                         scalar=WS, in1=wx_chunk(wx_hi, n), op0=ALU.mult, op1=ALU.subtract)\
                   .then_inc(s["w_lo"], 1)

            tasks = {"R": shift, "Q": q_lo, "K": k_lo_part, "V": v_lo_part, "A": out_lo, "N": normalise,
                     "O": accumulate, "X": lambda n, u: evict(dve, n, u)}
            dve.wait_ge(s["scales"], HQ)
            dve.wait_ge(s["attz"], 1)
            enter_bodies("DVE", {**tasks, "W": weights_lo}, 0, HALF)

            split_lo(dve, "wloD", ON_DVE[2:])

            blocks, first, end, first_slot = (per_e[:, i, :] for i in range(4))
            small(dve.tensor_scalar(ecmp[:, :, :], ecmp[:, :, :], 0.0, None, ALU.is_gt))
            dve.wait_ge(s["ranked"], 1)
            total = ps[4][:, RANK + NT * E:RANK + (NT + 1) * E]
            over = scratch[:, 0:TOK // BLK * E].rearrange("p (e j) -> p e j", e=E)
            small(dve.tensor_tensor(over, total.unsqueeze(2).to_broadcast([P, E, TOK // BLK]), steps[:, :, :],
                                    ALU.is_gt))
            small(dve.tensor_reduce(blocks, over, AX_X, ALU.add))
            before = scratch[:, 0:E * E].rearrange("p (e f) -> p e f", e=E)
            small(dve.tensor_tensor(before, blocks.unsqueeze(1).to_broadcast([P, E, E]), ecmp[:, :, :], ALU.mult))
            small(dve.tensor_reduce(first, before, AX_X, ALU.add))
            small(dve.tensor_tensor(end, first, blocks, ALU.add))
            small(dve.tensor_scalar(first_slot, first, float(BLK), None, ALU.mult))
            ended = scratch[:, :].rearrange("p (b e) -> p b e", e=E)
            small(dve.tensor_tensor(ended, block_no[:, :, :], end.unsqueeze(1).to_broadcast([P, NBLK, E]), ALU.is_ge))
            small(dve.tensor_reduce(blk_f[:, :], ended, AX_X, ALU.add))
            small(dve.tensor_scalar(blk_f[:, :], blk_f[:, :], E - 1.0, None, ALU.min))
            small(dve.tensor_copy(blk_expert[:, :], blk_f[0:1, :]))
            small(dve.tensor_tensor(cw, ps[4][:, RANK:RANK + NT * E].rearrange("p (t e) -> p t e", e=E),
                                    first_slot.unsqueeze(1).to_broadcast([P, NT, E]), ALU.add))
            for k, one in enumerate((one1, one2)):
                small(dve.tensor_tensor(t1, cw, one, ALU.mult))
                small(dve.tensor_reduce(slot_f[:, k, :], t1, AX_X, ALU.add))
            dve.tensor_copy(slot_of[:, :, :], slot_f[:, :, :]).then_inc(s["routed"], 1)

            weights_split(dve)
            dve.wait_ge(s["zeros"], 16 * ZERO_DMAS)
            run_bodies(dve, "DVE", {**tasks, "W": weights_lo}, 0, HALF)

            def inputs_lo(i, r):
                dve.wait_ge(s[f"gx_hi{r}"], i + 1)
                dve.tensor_tensor(xgT_lo[r], ps[6 + r][:, 0:BLK], xgT_hi[r], ALU.subtract)\
                   .then_inc(s[f"gx_lo{r}"], 1)

            def parts(i, r, g):
                h, hi, lo = (m[:, r, 2 * g:2 * g + 2, :] for m in (h32, h_hi, h_lo))
                dve.wait_ge(s[f"gelu{r}{g}"], i + 1)
                need(dve, f"ymm{r}", i)
                dve.tensor_copy(hi, h).then_inc(s[f"hhi{r}{g}"], 1)
                dve.wait_ge(s[f"hhi{r}{g}"], i + 1)
                dve.tensor_tensor(lo, h, hi, ALU.subtract).then_inc(s[f"hlo{r}{g}"], 1)

            def outputs(i, r):
                dve.wait_ge(s[f"ymm{r}"], i + 1)
                need(dve, f"ystore{r}", i * 16)
                dve.tensor_copy(y_sb[r], ps[4 + r][:, 0:BLK]).then_inc(s[f"yout{r}"], 1)

            for r in range(2):
                inputs_lo(0, r)
            for g in range(2):
                parts(0, 0, g)

            def steps_of(i):
                for r in range(2):
                    inputs_lo(i + 1, r)
                    for g in range(2):
                        parts(i + r, 1 - r, g)
                    outputs(i, r)

            steps_of(0)
            with dve.Fori(1, NBLK // 2 - 1) as i_:
                steps_of(i_)
            enter_bodies("DVE", {**tasks, "M": add_expert}, HALF, BODIES)
            for g in range(2):
                parts(NBLK // 2 - 1, 1, g)
            for r in range(2):
                outputs(NBLK // 2 - 1, r)

            run_bodies(dve, "DVE", {**tasks, "M": add_expert}, HALF, BODIES)

            dve.wait_ge(s["silu"], 1)
            dve.wait_ge(s["acc"], BODIES)
            for c in range(4):
                a, g, xx = (out_chunk(v, c) for v in (att, mix, X))
                dve.scalar_tensor_tensor(out=a, in0=a, scalar=1.0 / WS, in1=g, op0=ALU.mult, op1=ALU.mult)\
                   .then_inc(s["gated"], 1)
                if c >= 2:
                    dve.wait_ge(s["gated"], c + 1)
                    dve.tensor_tensor(xx, xx, a, ALU.add).then_inc(s["finD"], 1)


_INS = ["L0_attn_inputs", "L0_attn_W_qkv", "L0_attn_W_out", "L0_ffn_gate_w", "L0_ffn_gate_b",
        "L0_ffn_w1", "L0_ffn_b1", "L0_ffn_w2", "L0_ffn_b2"]


def kernel(**inputs):
    import numpy as _np
    import concourse.bacc as _bacc
    from concourse import mybir as _mybir
    from concourse.bass_utils import run_bass_kernel_spmd as _run

    nc = _bacc.Bacc("TRN2", target_bir_lowering=False, num_devices=1)
    arrays, args = {}, []
    for name in _INS:
        a = _np.ascontiguousarray(inputs[name])
        arrays[f"in_{name}"] = a
        args.append(nc.dram_tensor(f"in_{name}", a.shape, _mybir.dt.from_np(a.dtype), kind="ExternalInput").ap())
    out = nc.dram_tensor("out_x", (NB, SEQ, D), F32, kind="ExternalOutput").ap()
    build(nc, *args, out)
    r = _run(nc, [arrays], core_ids=[0])
    return r.results[0]["out_x"]
```
